# Optimizing a Trainium2 kernel written in Bass

```python
import numpy as np
import jax
import jax.numpy as jnp

def _softmax(x, axis=-1):
    return jax.nn.softmax(x, axis=axis)

def _gelu(x):
    return jax.nn.gelu(x, approximate=True)

def _silu(x):
    return jax.nn.silu(x)

def _sigmoid(x):
    return jax.nn.sigmoid(x)

def _layernorm(x, axis=-1, eps=1e-05):
    m = jnp.mean(x, axis=axis, keepdims=True)
    v = jnp.var(x, axis=axis, keepdims=True)
    return (x - m) / jnp.sqrt(v + eps)

def _scatter_add(tgt, idx, src, axis=0):
    return tgt.at[idx].add(src)

def _segment_sum(src, seg, n):
    return jax.ops.segment_sum(src, seg, n)
kernel_name = 'mk_flamingo_gated_d1_seqx_r8_c08eb0'

def setup_inputs(seed: int=0):
    np.random.seed(seed)
    _w = jnp.asarray

    def _rec_inputs():
        import jax
        import jax.numpy as jnp
        _rk = jax.random.key(seed)
        x = -0.0003929 + 0.9999 * jax.random.normal(jax.random.fold_in(_rk, 1), (64, 64, 128), jnp.float32)
        _lenS = 64 - jax.random.randint(jax.random.fold_in(_rk, 7), (64,), 0, max(1, 64 // 4) + 1, jnp.int32)
        _lenS2 = 64 - jax.random.randint(jax.random.fold_in(_rk, 8), (64,), 0, max(1, 64 // 4) + 1, jnp.int32)
        _ctx_512P = jax.random.normal(jax.random.fold_in(_rk, 11), (64, 16, 64), jnp.float32)
        _ctx_512c = jax.random.dirichlet(jax.random.fold_in(_rk, 511), 0.3 * jnp.ones((16,), jnp.float32), (64, 64))
        _ctx_512t = jnp.einsum('bsk,bkd->bsd', _ctx_512c, _ctx_512P)
        _ctx_512t = _ctx_512t * jax.lax.rsqrt(jnp.mean(jnp.square(_ctx_512t)) + 1e-12) * 0.953939
        ctx_512 = 4.13588e-05 + 0.999923 * (_ctx_512t + 0.3 * jax.random.normal(jax.random.fold_in(_rk, 611), (64, 64, 64), jnp.float32))
        _g = jax.random.normal(jax.random.fold_in(_rk, 9001), (2, 1), jnp.float32)
        _g = jnp.sign(_g) * jnp.maximum(jnp.abs(_g), 1.0) + (_g == 0) * 1.0
        g_xattn = _g[0]
        g_ffn = _g[1]
        return (x, ctx_512, g_xattn, g_ffn)
    x, ctx_512, g_xattn, g_ffn = _rec_inputs()

    def _L0_xattn_setup():
        import jax, jax.numpy as jnp
        import numpy as np
        B, LQ, LK = (8, 256, 256)
        QD, KD, VD = (128, 64, 64)
        key = jax.random.key(seed)
        ks = jax.random.split(key, 9)
        s = 0.02
        return {'query': jax.random.normal(ks[0], (B, LQ, QD), jnp.float32), 'key': jax.random.normal(ks[1], (B, LK, KD), jnp.float32), 'value': jax.random.normal(ks[2], (B, LK, VD), jnp.float32), 'Wq': jax.random.normal(ks[3], (QD, QD), jnp.float32) * s, 'bq': jnp.zeros((QD,), jnp.float32), 'Wk': jax.random.normal(ks[4], (KD, QD), jnp.float32) * s, 'bk': jnp.zeros((QD,), jnp.float32), 'Wv': jax.random.normal(ks[5], (VD, QD), jnp.float32) * s, 'bv': jnp.zeros((QD,), jnp.float32)}
    _L0_xattn_all = _L0_xattn_setup()
    _L0_xattn_in = {k: v for k, v in _L0_xattn_all.items() if k in ('Wq', 'bq', 'Wk', 'bk', 'Wv', 'bv')}
    del _L0_xattn_all

    def _L0_ffn_setup():
        import jax, jax.numpy as jnp
        import numpy as np
        B, S, H, FFN, E = (2, 256, 128, 512, 8)
        key = jax.random.key(seed)
        k0, k1, k2, k3 = jax.random.split(key, 4)
        return {'hidden_states': jax.random.normal(k0, (B, S, H), dtype=jnp.float32), 'Wr': jax.random.normal(k1, (H, E), dtype=jnp.float32) * 0.02, 'br': jnp.zeros((E,), dtype=jnp.float32), 'W1': jax.random.normal(k2, (E, H, FFN), dtype=jnp.float32) * 0.02, 'W2': jax.random.normal(k3, (E, FFN, H), dtype=jnp.float32) * 0.02}
    _L0_ffn_all = _L0_ffn_setup()
    _L0_ffn_in = {k: v for k, v in _L0_ffn_all.items() if k in ('Wr', 'br', 'W1', 'W2')}
    del _L0_ffn_all
    return {'x': x, 'ctx_512': ctx_512, 'g_xattn': g_xattn, 'g_ffn': g_ffn, 'L0_xattn_Wq': _L0_xattn_in['Wq'], 'L0_xattn_bq': _L0_xattn_in['bq'], 'L0_xattn_Wk': _L0_xattn_in['Wk'], 'L0_xattn_bk': _L0_xattn_in['bk'], 'L0_xattn_Wv': _L0_xattn_in['Wv'], 'L0_xattn_bv': _L0_xattn_in['bv'], 'L0_ffn_Wr': _L0_ffn_in['Wr'], 'L0_ffn_br': _L0_ffn_in['br'], 'L0_ffn_W1': _L0_ffn_in['W1'], 'L0_ffn_W2': _L0_ffn_in['W2']}

def reference(x, ctx_512, g_xattn, g_ffn, L0_xattn_Wq, L0_xattn_bq, L0_xattn_Wk, L0_xattn_bk, L0_xattn_Wv, L0_xattn_bv, L0_ffn_Wr, L0_ffn_br, L0_ffn_W1, L0_ffn_W2):
    import jax
    import jax.numpy as jnp

    def _L0_xattn_ref(query, key, value, Wq, bq, Wk, bk, Wv, bv):
        import jax, jax.numpy as jnp
        import numpy as np
        B, LQ, LK = (8, 256, 256)
        QD, KD, VD = (128, 64, 64)
        q = jnp.einsum('bld,de->ble', query, Wq) + bq
        k = jnp.einsum('bld,de->ble', key, Wk) + bk
        v = jnp.einsum('bld,de->ble', value, Wv) + bv
        scores = jnp.einsum('bqe,bke->bqk', q, k)
        attn = jax.nn.softmax(scores, axis=-1)
        out = jnp.einsum('bqk,bke->bqe', attn, v)
        return out

    def _L0_ffn_ref(hidden_states, Wr, br, W1, W2):
        import jax, jax.numpy as jnp
        import numpy as np
        B, S, H, FFN, E = (2, 256, 128, 512, 8)
        b, s, h = hidden_states.shape
        x = hidden_states.reshape(-1, h)
        route = jax.nn.sigmoid(x @ Wr + br)
        max_prob = jnp.max(route, axis=1, keepdims=True)
        max_ind = jnp.argmax(route, axis=1)
        out = jnp.zeros_like(x)
        n_experts = Wr.shape[1]
        for e in range(n_experts):
            mask = (max_ind == e)[:, None].astype(x.dtype)
            y = jax.nn.gelu(x @ W1[e], approximate=False) @ W2[e]
            out = out + mask * y
        out = out * max_prob
        return out.reshape(b, s, h)
    x = x + jnp.tanh(g_xattn[0]) * _L0_xattn_ref(_layernorm(x, axis=-1), ctx_512, ctx_512, L0_xattn_Wq, L0_xattn_bq, L0_xattn_Wk, L0_xattn_bk, L0_xattn_Wv, L0_xattn_bv)
    x = x + jnp.tanh(g_ffn[0]) * _L0_ffn_ref(_layernorm(x, axis=-1), L0_ffn_Wr, L0_ffn_br, L0_ffn_W1, L0_ffn_W2)
    return x

_drawn_inputs = setup_inputs


def setup_inputs(seed=0):
    import zlib

    import numpy as np

    out = dict(_drawn_inputs(seed))
    spreads = {'L0_xattn_bq': (0.0, 0.8),
     'L0_xattn_bk': (0.0, 0.8),
     'L0_xattn_bv': (0.0, 0.1),
     'L0_ffn_br': (0.0, 0.284)}
    factors = {'L0_xattn_Wq': 5.022, 'L0_xattn_Wk': 4.58}
    for name, (base, spread) in spreads.items():
        noise = np.random.default_rng([zlib.crc32(name.encode()), seed]).standard_normal(out[name].shape)
        drawn = base * np.exp(spread * noise) if base else spread * noise
        out[name] = jnp.asarray(drawn.astype(out[name].dtype))
    for name, factor in factors.items():
        out[name] = (out[name] * factor).astype(out[name].dtype)
    return out
```

```python
from contextlib import ExitStack

import concourse.bass as bass
from concourse import mybir

P = 128
F32 = mybir.dt.float32
BF16 = mybir.dt.bfloat16
I32 = mybir.dt.int32
ALU = mybir.AluOpType
ACT = mybir.ActivationFunctionType
AX = mybir.AxisListType

LN_EPS = 1e-5
GT = 4
CREDIT = 2
RING = 6

MEAN, RSTD, SCALE, TOKEN, ROW = 128, 129, 130, 131, 132


def nth(g):
    return g + 1 + CREDIT


def attention_moe(nc, x, ctx_in, g_xattn, g_ffn, Wq, bq, Wk, bk, Wv, bv, Wr, br, W1, W2, out):
    B, S, D = x.shape
    KD = ctx_in.shape[2]
    KA = KD + 1
    E, _, F = W1.shape
    N = B * S
    TILES = N // P
    NG = TILES // GT
    FC = F // P
    FFN_TILES = (N + E * (P - 1)) // P
    REGION = N + P
    SPARE = 2 * GT
    TABLE = -(-(FFN_TILES + 1) // RING)
    TW = 8
    assert D == P and S == 64 and KD == 64 and GT * P == 512 and NG % 2 == 0 and F == 512
    assert ROW == D + 4 and FFN_TILES - TILES <= SPARE

    scratch = nc.dram_tensor("scratch", (E * REGION + SPARE * P, ROW), F32, kind="Internal").ap()

    x_tok = x.rearrange("b s d -> (b s) d").rearrange("(t p) d -> p t d", p=P)
    ctx_tok = ctx_in.rearrange("b s d -> (b s) d").rearrange("(t p) d -> p t d", p=P)
    out_tok = out.rearrange("b s d -> (b s) d")

    with ExitStack() as stack:
        def sb(name, shape, dt=F32):
            return stack.enter_context(nc.sbuf_tensor(name, shape, dt))

        def sem(name):
            return stack.enter_context(nc.semaphore(name))

        x_all = sb("x_all", [P, TILES * D])
        w1_sb = sb("w1_sb", [P, E * F])
        w2_sb = sb("w2_sb", [P, E * FC * D])
        wq_sb = sb("wq_sb", [P, D])
        wk_sb = sb("wk_sb", [KA, D])
        wv_sb = sb("wv_sb", [KA, D])
        wvg_sb = sb("wvg_sb", [KA, D + 1])
        bq_col = sb("bq_col", [P, 1])
        wr_sb = sb("wr_sb", [P, E])
        br_sb = sb("br_sb", [P, E])
        gates = sb("gates", [P, 2])
        tanh_gates = sb("tanh_gates", [P, 2])
        ident = sb("ident", [P, P])
        before = sb("before", [P, P], BF16)
        ones_b = sb("ones_b", [P, P], BF16)
        minus_half = sb("minus_half", [P, GT])
        region_of = sb("region_of", [P, GT, E])
        first_wins = sb("first_wins", [P, GT, E])
        wqT_sb = sb("wqT_sb", [P, D])
        wkT_sb = sb("wkT_sb", [P, KA])
        wqk_sb = sb("wqk_sb", [P, KA])
        bqk_sb = sb("bqk_sb", [KA, 1])
        ctx_sb = [sb(f"ctx_{i}", [P, GT, KA]) for i in range(2)]
        stats1 = sb("stats1", [P, GT, 6])
        stats2 = sb("stats2", [P, GT, 6])
        mv1 = [sb(f"mv1_{i}", [P, GT, 2]) for i in range(2)]
        xn = [sb(f"xn_{i}", [P, GT, D]) for i in range(2)]
        xnT = [sb(f"xnT_{i}", [P, GT * P]) for i in range(2)]
        ctxT = [sb(f"ctxT_{i}", [KA, GT * P]) for i in range(2)]
        qT = [sb(f"qT_{i}", [KA, GT * P]) for i in range(2)]
        rowmax = sb("rowmax", [P, GT])
        shifted = [sb(f"shifted_{i}", [P, GT, S]) for i in range(2)]
        probs = [sb(f"probs_{i}", [P, GT, P]) for i in range(2)]
        probsT = [sb(f"probsT_{i}", [P, GT * P]) for i in range(2)]
        mixT = [sb(f"mixT_{i}", [KA, GT * P]) for i in range(2)]
        inv_sum = sb("inv_sum", [P, 2, GT // 2, 1])
        rows = [sb(f"rows_{i}", [P, GT, ROW]) for i in range(2)]
        x2n = [sb(f"x2n_{i}", [P, GT, D]) for i in range(2)]
        x2nT = [sb(f"x2nT_{i}", [P, GT * P]) for i in range(2)]
        logits = sb("logits", [P, GT, E])
        exp_neg = sb("exp_neg", [P, GT, E])
        one_plus = sb("one_plus", [P, GT, E])
        route = sb("route", [P, GT, E])
        route_max = [sb(f"route_max_{i}", [P, GT, 1]) for i in range(2)]
        is_max = sb("is_max", [P, GT, E])
        rank_max = sb("rank_max", [P, GT, E])
        best = sb("best", [P, GT, 1])
        onehot = [sb(f"onehot_{i}", [P, GT, E], BF16) for i in range(2)]
        group_sum = sb("group_sum", [P, E])
        so_far = [sb(f"so_far_{i}", [P, E], BF16) for i in range(2)]
        place = sb("place", [P, GT, E])
        place_of = sb("place_of", [P, GT, E])
        row_at = [sb(f"row_at_{i}", [P, GT, 1], I32) for i in range(2)]
        pad_rows = sb("pad_rows", [P, ROW])
        multiples = sb("multiples", [1, E, TILES])
        tile_no = sb("tile_no", [1, TABLE * TW, E])
        tile_row = sb("tile_row", [1, TABLE * TW])
        ones_e = sb("ones_e", [1, E])
        counts = sb("counts", [1, E])
        pad_at = sb("pad_at", [1, E], I32)
        full = sb("full", [1, E, TILES])
        n_tiles = sb("n_tiles", [1, E])
        end_tile = sb("end_tile", [1, E])
        passed = sb("passed", [1, TABLE * TW, E])
        passed_tiles = sb("passed_tiles", [1, TABLE * TW, E])
        expert = sb("expert", [1, TABLE * TW])
        first_tile = sb("first_tile", [1, TABLE * TW])
        row_raw = sb("row_raw", [1, TABLE * TW])
        tile_at = sb("tile_at", [1, TABLE * TW], I32)
        weights_at = sb("weights_at", [1, TABLE * TW], I32)
        tok = [sb(f"tok_{i}", [P, ROW]) for i in range(RING)]
        tokn = [sb(f"tokn_{i}", [P, D]) for i in range(2)]
        toknT = [sb(f"toknT_{i}", [P, P]) for i in range(2)]
        w1_now = [sb(f"w1_now_{i}", [P, F]) for i in range(2)]
        hT = [sb(f"hT_{i}", [P, F]) for i in range(2)]

        bank_xT = stack.enter_context(nc.psum_tensor("bank_xT", [P, 512], F32))
        bank_ctx = stack.enter_context(nc.psum_tensor("bank_ctx", [P, 512], F32))
        bank_q = stack.enter_context(nc.psum_tensor("bank_q", [P, 512], F32))
        bank_s = stack.enter_context(nc.psum_tensor("bank_s", [P, 512], F32))
        bank_p = stack.enter_context(nc.psum_tensor("bank_p", [P, 512], F32))
        bank_m = stack.enter_context(nc.psum_tensor("bank_m", [P, 512], F32))
        banks_o = stack.enter_context(nc.psum_tensor("banks_o", [P, 2, 512], F32))
        s_ps = bank_s[:, 0:GT * S].rearrange("p (t k) -> p t k", t=GT)
        lg_ps = bank_ctx[:, 0:GT * E].rearrange("p (t e) -> p t e", t=GT)
        pf_ps = bank_ctx[:, GT * E:2 * GT * E].rearrange("p (t e) -> p t e", t=GT)
        cnt_ps = bank_ctx[:, 0:E]
        o_ps = banks_o[:, :, 0:2 * (D + 1)].rearrange("p b (t c) -> p b t c", c=D + 1)
        wT_ps, wkT_ps = bank_p[:, 0:D], bank_p[:, D:D + KA]
        wqk_ps, bqk_ps = bank_m[:, 0:KA], bank_m[0:KA, KA:KA + 1]
        tT_ps = [bank_xT[:, 0:P], bank_ctx[:, 0:P]]
        h_ps = [bank_q, bank_p]
        y_ps = [banks_o[:, 0, 0:D], banks_o[:, 1, 0:D]]

        x_in = [sem("x_in0"), sem("x_in1"), sem("x_in_rest")]
        ctx_in_sem = [sem("ctx_in0"), sem("ctx_in1")]
        attn_w_in, route_w_in, expert_w_in = sem("attn_w_in"), sem("route_w_in"), sem("expert_w_in")
        zeroed, consts_ready, ids_ready, table_consts = (
            sem("zeroed"), sem("consts_ready"), sem("ids_ready"), sem("table_consts"))
        gates_ready, wv_ready = sem("gates_ready"), sem("wv_ready")
        wT_ready, wT_copied, folded, folded_copied = (
            sem("wT_ready"), sem("wT_copied"), sem("folded"), sem("folded_copied"))
        def stages(*names):
            return [sem(n) for n in names]

        by_dve = ln1_stats, xn_ready, shifted_ready, x2_ready, ln2_stats, x2n_ready, logits_ready, \
            onehot_ready, placed = stages("ln1_stats", "xn_ready", "shifted_ready", "x2_ready", "ln2_stats",
                                          "x2n_ready", "logits_ready", "onehot_ready", "placed")
        by_act = xnT_copied, ctxT_copied, qT_copied, probs_ready, probsT_copied, mixT_copied, x2nT_copied, \
            exp_ready = stages("xnT_copied", "ctxT_copied", "qT_copied", "probs_ready", "probsT_copied",
                               "mixT_copied", "x2nT_copied", "exp_ready")
        by_pe = xnT_done, ctxT_done, qT_done, scores_done, probsT_done, mix_done, attn_done, x2nT_done, \
            logits_done, prefix_done = stages("xnT_done", "ctxT_done", "qT_done", "scores_done", "probsT_done",
                                              "mix_done", "attn_done", "x2nT_done", "logits_done", "prefix_done")
        by_pool = rstd1_ready, rstd2_ready = stages("rstd1_ready", "rstd2_ready")
        scattered = [sem("scattered0"), sem("scattered1")]
        bn1, bn2, max_done, sums_done, routing = (
            sem("bn1"), sem("bn2"), sem("max_done"), sem("sums_done"), sem("routing"))
        ROUTING = 10
        eps1, eps2, pool_step = sem("eps1"), sem("eps2"), sem("pool_step")
        wait_over = sem("wait_over")
        counts_done, counts_copied, pad_at_ready, table_step, table_ready, pads_written = (
            sem("counts_done"), sem("counts_copied"), sem("pad_at_ready"), sem("table_step"),
            sem("table_ready"), sem("pads_written"))
        pads_ready = sem("pads_ready")
        tok_in = [sem(f"tok_in{i}") for i in range(RING)]
        tok_out = [sem(f"tok_out{i}") for i in range(RING)]
        ffn_dve = tokn_ready, toknT_copied, y_added = stages("tokn_ready", "toknT_copied", "y_added")
        ffn_pe = toknT_done, h_done, y_done = stages("toknT_done", "h_done", "y_done")
        gelu_done, w1_copied = sem("gelu_done"), sem("w1_copied")

        def steps(eng, body):
            for k in (0, 1):
                body(k, k // 2, k % 2)
            with eng.Fori(1, NG // 2) as i:
                for u in (0, 1):
                    body(i * 2 + u, i, u)
            for k in (NG, NG + 1):
                body(k, k // 2, k % 2)

        def live(k, lag):
            return not isinstance(k, int) or 0 <= k - lag < NG

        LOOPS = FFN_TILES // RING

        def tiles(eng, body, iteration=None, last=None):
            with eng.Fori(0, LOOPS) as i:
                if iteration:
                    iteration(i)
                for u in range(RING):
                    body(i * RING + u, i, u)
            if last:
                last()
            for j in range(LOOPS * RING, FFN_TILES):
                body(j, LOOPS, j % RING)

        def give_credit(eng, sems):
            for s in sems:
                eng.sem_inc(s, CREDIT)

        def wait_apart(eng, s, count):
            eng.wait_ge(s, count)
            eng.sem_inc(wait_over, 1)

        block = stack.enter_context(nc.Block())

        @block.sync
        def _(sp):
            def load_x(g0, g1, which):
                sp.dma_start(x_all[:, g0 * GT * D:g1 * GT * D].rearrange("p (t d) -> p t d", d=D),
                             x_tok[:, g0 * GT:g1 * GT, :]).then_inc(x_in[which], 16)

            def load_ctx(g, p):
                sp.dma_start(ctx_sb[p][:, :, 0:KD], ctx_tok[:, bass.ds(g * GT, GT), :]).then_inc(ctx_in_sem[p], 16)

            def load_expert(e):
                sp.dma_start(w1_sb[:, bass.ds(e * F, F)], W1.rearrange("e p f -> p e f")[:, bass.ds(e, 1), :]
                             .rearrange("p a f -> p (a f)")).then_inc(expert_w_in, 16)
                sp.dma_start(w2_sb[:, bass.ds(e * F, F)].rearrange("p (c d) -> p c d", d=D),
                             W2.rearrange("e (c p) d -> p (e c) d", p=P)[:, bass.ds(e * FC, FC), :]
                             ).then_inc(expert_w_in, 16)

            load_x(0, 1, 0)
            sp.dma_start(wq_sb[:], Wq).then_inc(attn_w_in, 16)
            sp.dma_start(wk_sb[0:KD, :], Wk).then_inc(attn_w_in, 16)
            sp.dma_start(wk_sb[KD:KA, :], bk.rearrange("(a d) -> a d", a=1)).then_inc(attn_w_in, 16)
            sp.dma_start(wv_sb[0:KD, :], Wv).then_inc(attn_w_in, 16)
            sp.dma_start(wv_sb[KD:KA, :], bv.rearrange("(a d) -> a d", a=1)).then_inc(attn_w_in, 16)
            sp.dma_start(bq_col[:], bq.rearrange("(d a) -> d a", a=1)).then_inc(attn_w_in, 16)
            sp.dma_start(gates[:, 0:1], g_xattn.partition_broadcast(P)).then_inc(attn_w_in, 16)
            sp.dma_start(gates[:, 1:2], g_ffn.partition_broadcast(P)).then_inc(attn_w_in, 16)
            load_ctx(0, 0)
            load_x(1, 2, 1)
            load_ctx(1, 1)
            sp.dma_start(wr_sb[:], Wr).then_inc(route_w_in, 16)
            sp.dma_start(br_sb[:], br.partition_broadcast(P)).then_inc(route_w_in, 16)
            load_x(2, NG, 2)
            for e in range(E - NG + 2):
                load_expert(e)
            with sp.Fori(1, NG // 2) as i:
                for u in (0, 1):
                    g = i * 2 + u
                    sp.wait_ge(mix_done, nth(g - 2))
                    load_ctx(g, u)
                    load_expert(g + (E - NG))
            sp.wait_ge(pads_ready, 1)
            sp.wait_ge(pad_at_ready, 1)
            regs = [sp.alloc_register(f"pad{e}") for e in range(E)]
            sp.reg_load(regs, pad_at[0:1, :])
            for e in range(E):
                at = sp.snap(regs[e], min_val=e * REGION, max_val=e * REGION + N)
                sp.dma_start(scratch[bass.ds(at, P), :], pad_rows[:]).then_inc(pads_written, 16)

            sp.wait_ge(table_ready, 1)
            for p in range(2):
                sp.wait_ge(scattered[p], 16 * GT * (NG // 2 + 1))
            sp.wait_ge(pads_written, 16 * E)
            at_regs = [sp.alloc_register(f"tile{m}") for m in range(RING)]

            def tile_rows(i, n):
                sp.reg_load(at_regs[0:n], tile_at[0:1, bass.ds(i * TW, n)])
                return [sp.snap(r, min_val=0, max_val=E * REGION + (SPARE - 1) * P) for r in at_regs[0:n]]

            def load_tile(at, u):
                sp.dma_start(tok[u][:], scratch[bass.ds(at, P), :]).then_inc(tok_in[u], 16)

            for u, at in enumerate(tile_rows(0, RING)):
                load_tile(at, u)
            with sp.Fori(1, LOOPS) as i:
                for u, at in enumerate(tile_rows(i, RING)):
                    sp.wait_ge(tok_out[u], i * 16)
                    load_tile(at, u)
            for u, at in enumerate(tile_rows(LOOPS, FFN_TILES - LOOPS * RING)):
                sp.wait_ge(tok_out[u], LOOPS * 16)
                load_tile(at, u)
            for u in range(RING):
                sp.wait_ge(tok_out[u], 16 * (LOOPS + (u < FFN_TILES - LOOPS * RING)))

        @block.gpsimd
        def _(pool):
            give_credit(pool, by_pool)
            nc.gpsimd.memset(ident[:], 0.0).then_inc(zeroed, 1)
            nc.gpsimd.memset(before[:], 0.0).then_inc(zeroed, 1)
            pool.wait_ge(zeroed, 2)
            nc.gpsimd.affine_select(out=ident[:], in_=ident[:], compare_op=ALU.not_equal, fill=1.0, base=0,
                                    pattern=[[-1, P]], channel_multiplier=1).then_inc(consts_ready, 1)
            nc.gpsimd.memset(minus_half[:], -0.5)
            nc.gpsimd.memset(ctx_sb[0][:, :, KD:KA], 1.0)
            nc.gpsimd.memset(ctx_sb[1][:, :, KD:KA], 1.0)
            nc.gpsimd.memset(probs[0][:], 0.0)
            nc.gpsimd.memset(probs[1][:], 0.0).then_inc(consts_ready, 1)
            nc.gpsimd.affine_select(out=before[:], in_=before[:], compare_op=ALU.is_ge, fill=1.0, base=0,
                                    pattern=[[-1, P]], channel_multiplier=1)
            nc.gpsimd.memset(ones_b[:], 1.0)
            nc.gpsimd.memset(so_far[0][:], 0.0)
            nc.gpsimd.iota(region_of[:], [[0, GT], [REGION, E]], base=0, channel_multiplier=0,
                           allow_small_or_imprecise_dtypes=True)
            nc.gpsimd.iota(first_wins[:], [[0, GT], [-1, E]], base=E, channel_multiplier=0,
                           allow_small_or_imprecise_dtypes=True).then_inc(consts_ready, 1)
            for p in range(2):
                nc.gpsimd.iota(rows[p][:, :, TOKEN:ROW].bitcast(I32), [[P, GT]], base=(p - 2) * GT * P,
                               channel_multiplier=1).then_inc(ids_ready, 1)

            nc.gpsimd.memset(pad_rows[:, 0:TOKEN], 0.0)
            nc.gpsimd.iota(pad_rows[:, TOKEN:ROW].bitcast(I32), [[0, 1]], base=N,
                           channel_multiplier=0).then_inc(pads_ready, 1)

            def write_spares():
                pool.wait_ge(pads_ready, 1)
                for p in range(2):
                    for t in range(GT):
                        at = E * REGION + (p * GT + t) * P
                        pool.dma_start(scratch[at:at + P, :], pad_rows[:]).then_inc(scattered[p], 16)

            def table_constants():
                nc.gpsimd.iota(multiples[:], [[0, E], [P, TILES]], base=0, channel_multiplier=0,
                               allow_small_or_imprecise_dtypes=True)
                nc.gpsimd.iota(tile_no[:], [[RING, TABLE], [1, TW], [0, E]], base=0, channel_multiplier=0,
                               allow_small_or_imprecise_dtypes=True)
                nc.gpsimd.iota(tile_row[:], [[RING * P, TABLE], [P, TW]], base=0, channel_multiplier=0,
                               allow_small_or_imprecise_dtypes=True)
                nc.gpsimd.memset(ones_e[:], 1.0).then_inc(table_consts, 1)

            def rstd(var, g, done, link, source):
                wait_apart(pool, source, nth(g))
                nc.gpsimd.tensor_scalar(var, var, LN_EPS, None, ALU.add).then_inc(link, 1)
                wait_apart(pool, link, g + 1)
                nc.gpsimd.tensor_tensor(var, var, minus_half[:].unsqueeze(2), ALU.pow).then_inc(done, 1)

            def scatter_rows(g, half, p):
                wait_apart(pool, scattered[p], 16 * GT * (half + 1))
                ids = rows[p][:, :, TOKEN:ROW].bitcast(I32)
                nc.gpsimd.tensor_scalar(ids, ids, float(2 * GT * P), None, ALU.add)
                wait_apart(pool, placed, nth(g))
                nc.gpsimd.tensor_scalar(rows[p][:, :, SCALE:TOKEN], route_max[p][:], tanh_gates[:, 1:2], None,
                                        ALU.mult).then_inc(pool_step, 1)
                pool.wait_ge(pool_step, g + 1)
                wait_apart(pool, rstd2_ready, nth(g))
                for t in range(GT):
                    nc.gpsimd.indirect_dma_start(
                        out=scratch, out_offset=bass.IndirectOffsetOnAxis(ap=row_at[p][:, t, :], axis=0),
                        in_=rows[p][:, t, :], in_offset=None).then_inc(scattered[p], 16)

            pool.wait_ge(ids_ready, 2)
            pool.wait_ge(gates_ready, 1)

            def body(k, i, u):
                if live(k, 0):
                    rstd(mv1[u][:, :, 1:2], k, rstd1_ready, eps1, ln1_stats)
                if live(k, 2):
                    scatter_rows(k - 2, i - 1, u)
                if live(k, 1):
                    rstd(rows[1 - u][:, :, RSTD:SCALE], k - 1, rstd2_ready, eps2, ln2_stats)
                if isinstance(k, int) and k == 0:
                    write_spares()
                if isinstance(k, int) and k == 1:
                    table_constants()

            steps(pool, body)

            def scatter_tile(j, i, u):
                wait_apart(pool, y_added, nth(j))
                nc.gpsimd.indirect_dma_start(
                    out=out_tok, out_offset=bass.IndirectOffsetOnAxis(ap=tok[u][:, TOKEN:ROW].bitcast(I32), axis=0),
                    in_=tok[u][:, 0:D], in_offset=None, bounds_check=N - 1, oob_is_err=False).then_inc(tok_out[u], 16)

            tiles(pool, scatter_tile)

        @block.scalar
        def _(act):
            give_credit(act, by_act)
            act.sem_inc(gelu_done, CREDIT)
            act.wait_ge(attn_w_in, 16 * 8)
            nc.scalar.activation(tanh_gates[:], gates[:], ACT.Tanh).then_inc(gates_ready, 1)

            def body(k, i, u):
                def evacuate(dst, src, filled, freed, copied, g):
                    act.wait_ge(filled, nth(g))
                    act.wait_ge(freed, nth(g - 2))
                    nc.scalar.copy(dst, src).then_inc(copied, 1)

                if live(k, 2):
                    evacuate(x2nT[u][:], bank_xT[:], x2nT_done, logits_done, x2nT_copied, k - 2)
                if live(k, 1):
                    v = 1 - u
                    act.wait_ge(shifted_ready, nth(k - 1))
                    act.wait_ge(probsT_done, nth(k - 3))
                    nc.scalar.activation(probs[v][0:S, :, 0:S], shifted[v][0:S], ACT.Exp)
                    nc.scalar.activation(probs[v][S:P, :, S:P], shifted[v][S:P], ACT.Exp).then_inc(probs_ready, 1)
                if live(k, 0):
                    evacuate(xnT[u][:], bank_xT[:], xnT_done, qT_done, xnT_copied, k)
                if live(k, 2):
                    act.wait_ge(logits_ready, nth(k - 2))
                    act.wait_ge(onehot_ready, nth(k - 3))
                    nc.scalar.activation(exp_neg[:], logits[:], ACT.Exp, scale=-1.0).then_inc(exp_ready, 1)
                if live(k, 1):
                    evacuate(probsT[1 - u][:], bank_p[:], probsT_done, mix_done, probsT_copied, k - 1)
                if live(k, 0):
                    evacuate(ctxT[u][:], bank_ctx[0:KA, :], ctxT_done, scores_done, ctxT_copied, k)
                if live(k, 0):
                    act.wait_ge(qT_done, nth(k))
                    act.wait_ge(scores_done, nth(k - 2))
                    nc.scalar.activation(qT[u][:], bank_q[0:KA, :], ACT.Identity,
                                         bias=bqk_sb[:, 0:1]).then_inc(qT_copied, 1)
                if live(k, 1):
                    evacuate(mixT[1 - u][:], bank_m[0:KA, :], mix_done, attn_done, mixT_copied, k - 1)

            act.wait_ge(folded_copied, 2)
            steps(act, body)

            def gelu(j, i, u):
                act.wait_ge(h_done, nth(j))
                act.wait_ge(y_done, nth(j - 2))
                nc.scalar.activation(hT[u % 2][:], h_ps[u % 2][:], ACT.Gelu).then_inc(gelu_done, 1)

            tiles(act, gelu)

        @block.vector
        def _(dve):
            give_credit(dve, by_dve)
            give_credit(dve, ffn_dve)
            dve.wait_ge(attn_w_in, 16 * 8)
            dve.wait_ge(gates_ready, 1)
            dve.wait_ge(consts_ready, 2)
            nc.vector.tensor_scalar(wvg_sb[:, 0:D], wv_sb[:], tanh_gates[0:KA, 0:1], None, ALU.mult)
            nc.vector.memset(wvg_sb[0:KD, D:D + 1], 0.0)
            nc.vector.memset(wvg_sb[KD:KA, D:D + 1], 1.0).then_inc(wv_ready, 1)
            dve.wait_ge(wT_ready, 1)
            nc.vector.tensor_copy(wqT_sb[:], wT_ps)
            nc.vector.tensor_copy(wkT_sb[:], wkT_ps).then_inc(wT_copied, 1)
            dve.wait_ge(folded, 1)
            nc.vector.tensor_copy(wqk_sb[:], wqk_ps).then_inc(folded_copied, 1)
            nc.vector.tensor_copy(bqk_sb[:], bqk_ps).then_inc(folded_copied, 1)

            def x_of(g, t):
                return x_all[:, bass.ds(g * (GT * D) + t * D, D)]

            def layer_stats1(g, p):
                for t in range(GT):
                    last = nc.vector.bn_stats(stats1[:, t, :], x_of(g, t))
                last.then_inc(bn1, 1)
                wait_apart(dve, bn1, g + 1)
                for t in range(GT):
                    last = nc.vector.bn_aggr(mv1[p][:, t, :], stats1[:, t, :])
                last.then_inc(ln1_stats, 1)

            def normalise1(g, p):
                dve.wait_ge(rstd1_ready, nth(g))
                dve.wait_ge(xnT_done, nth(g - 2))
                for t in range(GT):
                    last = nc.vector.tensor_scalar(xn[p][:, t, :], x_of(g, t), mv1[p][:, t, 0:1],
                                                   mv1[p][:, t, 1:2], ALU.subtract, ALU.mult)
                last.then_inc(xn_ready, 1)

            def softmax_shift(g, p):
                dve.wait_ge(scores_done, nth(g))
                nc.vector.tensor_reduce(rowmax[:], s_ps, AX.X, ALU.max).then_inc(max_done, 1)
                dve.wait_ge(max_done, g + 1)
                dve.wait_ge(probs_ready, nth(g - 2))
                nc.vector.tensor_tensor(shifted[p][:], s_ps, rowmax[:].unsqueeze(2).broadcast_to([P, GT, S]),
                                        ALU.subtract).then_inc(shifted_ready, 1)

            def residual1(g, half, p):
                dve.wait_ge(attn_done, nth(g))
                nc.vector.reciprocal(inv_sum[:], o_ps[:, :, :, D:D + 1]).then_inc(sums_done, 1)
                dve.wait_ge(sums_done, g + 1)
                dve.wait_ge(scattered[p], 16 * GT * (half + 1))
                for t in range(GT):
                    last = nc.vector.scalar_tensor_tensor(
                        out=rows[p][:, t, 0:D], in0=o_ps[:, t // 2, t % 2, 0:D],
                        scalar=inv_sum[:, t // 2, t % 2, :], in1=x_of(g, t), op0=ALU.mult, op1=ALU.add)
                last.then_inc(x2_ready, 1)
                dve.wait_ge(x2_ready, nth(g))
                for t in range(GT):
                    last = nc.vector.bn_stats(stats2[:, t, :], rows[p][:, t, 0:D])
                last.then_inc(bn2, 1)
                wait_apart(dve, bn2, g + 1)
                for t in range(GT):
                    last = nc.vector.bn_aggr(rows[p][:, t, MEAN:SCALE], stats2[:, t, :])
                last.then_inc(ln2_stats, 1)

            def normalise2(g, p):
                dve.wait_ge(rstd2_ready, nth(g))
                dve.wait_ge(x2nT_done, nth(g - 2))
                for t in range(GT):
                    last = nc.vector.tensor_scalar(x2n[p][:, t, :], rows[p][:, t, 0:D], rows[p][:, t, MEAN:RSTD],
                                                   rows[p][:, t, RSTD:SCALE], ALU.subtract, ALU.mult)
                last.then_inc(x2n_ready, 1)

            def add_bias(g):
                dve.wait_ge(logits_done, nth(g))
                dve.wait_ge(exp_ready, nth(g - 1))
                nc.vector.tensor_tensor(logits[:], lg_ps, br_sb[:].unsqueeze(1).broadcast_to([P, GT, E]),
                                        ALU.add).then_inc(logits_ready, 1)

            def choose(g, p):
                def link(ins, n):
                    ins.then_inc(routing, 1)
                    dve.wait_ge(routing, g * ROUTING + n)

                wide = [P, GT, E]
                dve.wait_ge(exp_ready, nth(g))
                link(nc.vector.tensor_scalar(one_plus[:], exp_neg[:], 1.0, None, ALU.add), 1)
                link(nc.vector.reciprocal(route[:], one_plus[:]), 2)
                link(nc.vector.tensor_reduce(route_max[p][:], route[:], AX.X, ALU.max), 3)
                link(nc.vector.tensor_tensor(is_max[:], route[:], route_max[p][:].broadcast_to(wide), ALU.is_equal), 4)
                link(nc.vector.tensor_tensor(rank_max[:], is_max[:], first_wins[:], ALU.mult), 5)
                link(nc.vector.tensor_reduce(best[:], rank_max[:], AX.X, ALU.max), 6)
                dve.wait_ge(prefix_done, nth(g - 1))
                link(nc.vector.tensor_tensor(onehot[p][:], rank_max[:], best[:].broadcast_to(wide), ALU.is_equal), 7)
                link(nc.vector.tensor_reduce(group_sum[:], onehot[p][:].rearrange("p t e -> p e t"), AX.X, ALU.add), 8)
                nc.vector.tensor_tensor(so_far[1 - p][:], so_far[p][:], group_sum[:], ALU.add).then_inc(onehot_ready, 1)

            def place_rows(g, p):
                dve.wait_ge(prefix_done, nth(g))
                nc.vector.tensor_tensor(place[:], pf_ps, region_of[:], ALU.add).then_inc(routing, 1)
                dve.wait_ge(routing, g * ROUTING + 9)
                nc.vector.tensor_tensor(place_of[:], place[:], onehot[p][:], ALU.mult).then_inc(routing, 1)
                dve.wait_ge(routing, g * ROUTING + 10)
                with nc.allow_low_precision(reason="whole numbers below 2**24 are exact"):
                    nc.vector.tensor_reduce(row_at[p][:], place_of[:], AX.X, ALU.add).then_inc(placed, 1)

            def body(k, i, u):
                v = 1 - u
                if live(k, 2):
                    normalise2(k - 2, u)
                if live(k, 0):
                    if isinstance(k, int):
                        dve.wait_ge(x_in[k], 16)
                    else:
                        dve.wait_ge(x_in[2], 16)
                    layer_stats1(k, u)
                if live(k, 1):
                    softmax_shift(k - 1, v)
                if live(k, 0):
                    normalise1(k, u)
                if live(k, 2):
                    add_bias(k - 2)
                    choose(k - 2, u)
                if live(k, 1):
                    residual1(k - 1, i + (u - 1) // 2, v)
                if live(k, 2):
                    place_rows(k - 2, u)

            dve.wait_ge(consts_ready, 3)
            dve.wait_ge(route_w_in, 32)
            steps(dve, body)

            table = [0]

            def link(ins):
                table[0] += 1
                ins.then_inc(table_step, 1)
                dve.wait_ge(table_step, table[0])

            deep = [1, TABLE * TW, E]
            dve.wait_ge(table_consts, 1)
            dve.wait_ge(counts_done, 1)
            link(nc.vector.tensor_copy(counts[:], cnt_ps[0:1, :]))
            nc.vector.tensor_tensor(pad_at[:], counts[:], region_of[0:1, 0, :], ALU.add).then_inc(pad_at_ready, 1)
            link(nc.vector.tensor_tensor(full[:], counts[:].unsqueeze(2).broadcast_to([1, E, TILES]), multiples[:],
                                         ALU.is_gt))
            link(nc.vector.tensor_reduce(n_tiles[:], full[:], AX.X, ALU.add))
            link(nc.vector.tensor_tensor_scan(end_tile[:], ones_e[:], n_tiles[:], 0.0, ALU.mult, ALU.add))
            link(nc.vector.tensor_tensor(passed[:], end_tile[:].unsqueeze(1).broadcast_to(deep), tile_no[:], ALU.is_le))
            link(nc.vector.tensor_reduce(expert[:], passed[:], AX.X, ALU.add))
            link(nc.vector.tensor_tensor(passed_tiles[:], passed[:], n_tiles[:].unsqueeze(1).broadcast_to(deep), ALU.mult))
            link(nc.vector.tensor_reduce(first_tile[:], passed_tiles[:], AX.X, ALU.add))
            nc.vector.tensor_scalar(weights_at[:], expert[:], float(E - 1), float(F), ALU.min, ALU.mult)
            link(nc.vector.scalar_tensor_tensor(out=row_raw[:], in0=expert[:], scalar=float(REGION), in1=tile_row[:],
                                                op0=ALU.mult, op1=ALU.add))
            nc.vector.scalar_tensor_tensor(out=tile_at[:], in0=first_tile[:], scalar=float(-P), in1=row_raw[:],
                                           op0=ALU.mult, op1=ALU.add).then_inc(table_ready, 1)

            def normalise_tile(j, i, u):
                dve.wait_ge(tok_in[u], i * 16 + 16)
                dve.wait_ge(toknT_done, nth(j - 2))
                nc.vector.tensor_scalar(tokn[u % 2][:], tok[u][:, 0:D], tok[u][:, MEAN:RSTD], tok[u][:, RSTD:SCALE],
                                        ALU.subtract, ALU.mult).then_inc(tokn_ready, 1)

            def copy_transposed(j, u):
                dve.wait_ge(toknT_done, nth(j))
                dve.wait_ge(h_done, nth(j - 2))
                nc.vector.tensor_copy(toknT[u % 2][:], tT_ps[u % 2]).then_inc(toknT_copied, 1)

            def copy_w1(u, at):
                nc.vector.tensor_copy(w1_now[u % 2][:], w1_sb[:, bass.ds(at, F)]).then_inc(w1_copied, 1)

            def residual2(j, u):
                dve.wait_ge(y_done, nth(j))
                nc.vector.scalar_tensor_tensor(out=tok[u][:, 0:D], in0=y_ps[u % 2], scalar=tok[u][:, SCALE:TOKEN],
                                               in1=tok[u][:, 0:D], op0=ALU.mult, op1=ALU.add).then_inc(y_added, 1)

            w_regs = [dve.alloc_register(f"wd{m}") for m in range(TW)]
            w_at = []

            def experts_of(i):
                dve.reg_load(w_regs, weights_at[0:1, bass.ds(i * TW, TW)])
                w_at[:] = [dve.snap(r, min_val=0, max_val=(E - 1) * F) for r in w_regs]

            dve.wait_ge(table_ready, 1)
            dve.wait_ge(expert_w_in, 16 * 2 * E)
            experts_of(0)
            copy_w1(0, w_at[0])
            copy_w1(1, w_at[1])
            normalise_tile(0, 0, 0)
            normalise_tile(1, 0, 1)
            copy_transposed(0, 0)
            copy_transposed(1, 1)
            normalise_tile(2, 0, 2)

            def tile(j, i, u):
                if not isinstance(j, int) or j + 2 < FFN_TILES:
                    copy_transposed(j + 2, u + 2)
                    copy_w1(u + 2, w_at[u + 2])
                if not isinstance(j, int) or j + 3 < FFN_TILES:
                    normalise_tile(j + 3, i + (u + 3) // RING, (u + 3) % RING)
                residual2(j, u)

            tiles(dve, tile, iteration=experts_of, last=lambda: experts_of(LOOPS))

        @block.tensor
        def _(pe):
            give_credit(pe, by_pe)
            give_credit(pe, ffn_pe)
            pe.wait_ge(consts_ready, 2)
            pe.wait_ge(attn_w_in, 16 * 8)
            nc.tensor.transpose(wT_ps, wq_sb[:], ident[:])
            nc.tensor.transpose(wkT_ps, wk_sb[:], ident[0:KA, 0:KA]).then_inc(wT_ready, 1)
            pe.wait_ge(wT_copied, 1)
            nc.tensor.matmul(wqk_ps, wqT_sb[:], wkT_sb[:], start=True, stop=True)
            nc.tensor.matmul(bqk_ps, wkT_sb[:], bq_col[:], start=True, stop=True).then_inc(folded, 1)
            pe.wait_ge(folded_copied, 2)
            pe.wait_ge(wv_ready, 1)

            def transposes(dst, src, done):
                for t in range(GT):
                    last = nc.tensor.transpose(dst[:, t * P:(t + 1) * P], src[:, t, :], ident[:])
                last.then_inc(done, 1)

            def scores(g, p):
                pe.wait_ge(qT_copied, nth(g))
                pe.wait_ge(ctxT_copied, nth(g))
                pe.wait_ge(shifted_ready, nth(g - 1))
                for t in range(GT):
                    for b in range(2):
                        cols = slice(t * P + b * S, t * P + b * S + S)
                        last = nc.tensor.matmul(s_ps[b * S:b * S + S, t, :], qT[p][:, cols], ctxT[p][:, cols],
                                                start=True, stop=True)
                last.then_inc(scores_done, 1)

            def prefix(g, p):
                pe.wait_ge(onehot_ready, nth(g))
                pe.wait_ge(ctxT_copied, nth(min(g + 2, NG - 1) if isinstance(g, int) else g + 2))
                nc.tensor.matmul(pf_ps, before[:], onehot[p][:], start=True, stop=False)
                for t in range(GT - 1):
                    nc.tensor.matmul(pf_ps[:, t + 1:GT, :], ones_b[:],
                                     onehot[p][:, t:t + 1, :].broadcast_to([P, GT - 1 - t, E]),
                                     start=False, stop=False)
                nc.tensor.matmul(pf_ps, ones_b[:], so_far[p][:].unsqueeze(1).broadcast_to([P, GT, E]),
                                 start=False, stop=True).then_inc(prefix_done, 1)

            def body(k, i, u):
                v = 1 - u
                static = isinstance(k, int)
                if live(k, 2):
                    pe.wait_ge(x2n_ready, nth(k - 2))
                    pe.wait_ge(xnT_copied, nth(min(k - 1, NG - 1) if static else k - 1))
                    transposes(bank_xT, x2n[u], x2nT_done)
                if live(k, 1):
                    scores(k - 1, v)
                if live(k, 2):
                    pe.wait_ge(x2nT_copied, nth(k - 2))
                    pe.wait_ge(placed, max(nth(k - 3), 1) if static else nth(k - 3))
                    for t in range(GT):
                        last = nc.tensor.matmul(lg_ps[:, t, :], x2nT[u][:, t * P:(t + 1) * P], wr_sb[:],
                                                start=True, stop=True)
                    last.then_inc(logits_done, 1)
                if live(k, 0):
                    pe.wait_ge(xn_ready, nth(k))
                    pe.wait_ge(x2nT_copied, nth(k - 2))
                    transposes(bank_xT, xn[u], xnT_done)
                if live(k, 1):
                    pe.wait_ge(probs_ready, nth(k - 1))
                    pe.wait_ge(probsT_copied, nth(k - 2))
                    transposes(bank_p, probs[v], probsT_done)
                if live(k, 0):
                    pe.wait_ge(ctx_in_sem[u], i * 16 + 16)
                    pe.wait_ge(placed, max(nth(k - 3), 1) if static else nth(k - 3))
                    pe.wait_ge(logits_ready, nth(k - 2))
                    transposes(bank_ctx[0:KA, :], ctx_sb[u], ctxT_done)
                if live(k, 0):
                    pe.wait_ge(xnT_copied, nth(k))
                    pe.wait_ge(qT_copied, nth(k - 1))
                    nc.tensor.matmul(bank_q[0:KA, :], wqk_sb[:], xnT[u][:], start=True, stop=True).then_inc(qT_done, 1)
                if live(k, 1):
                    pe.wait_ge(probsT_copied, nth(k - 1))
                    pe.wait_ge(mixT_copied, nth(k - 2))
                    for t in range(GT):
                        last = nc.tensor.matmul(bank_m[0:KA, t * P:(t + 1) * P], ctx_sb[v][:, t, :],
                                                probsT[v][:, t * P:(t + 1) * P], start=True, stop=True)
                    last.then_inc(mix_done, 1)
                if live(k, 2):
                    prefix(k - 2, u)
                if live(k, 1):
                    pe.wait_ge(mixT_copied, nth(k - 1))
                    pe.wait_ge(x2_ready, nth(k - 2))
                    for t in range(GT):
                        last = nc.tensor.matmul(o_ps[:, t // 2, t % 2, :], mixT[v][:, t * P:(t + 1) * P], wvg_sb[:],
                                                start=True, stop=True)
                    last.then_inc(attn_done, 1)

            pe.wait_ge(consts_ready, 3)
            pe.wait_ge(route_w_in, 32)
            steps(pe, body)

            pe.wait_ge(placed, nth(NG - 1))
            nc.tensor.matmul(cnt_ps, ones_b[:], so_far[NG % 2][:], start=True, stop=True).then_inc(counts_done, 1)

            w_regs = [pe.alloc_register(f"w{m}") for m in range(RING)]
            w_at = []

            def experts_of(i):
                pe.reg_load(w_regs, weights_at[0:1, bass.ds(i * TW, RING)])
                w_at[:] = [pe.snap(r, min_val=0, max_val=(E - 1) * F) for r in w_regs]

            def transpose_tile(j, u):
                pe.wait_ge(tokn_ready, nth(j))
                pe.wait_ge(toknT_copied, nth(j - 2))
                nc.tensor.transpose(tT_ps[u % 2], tokn[u % 2][:], ident[:]).then_inc(toknT_done, 1)

            def up(j, u):
                pe.wait_ge(toknT_copied, nth(j))
                pe.wait_ge(w1_copied, j + 1)
                pe.wait_ge(gelu_done, nth(j - 2))
                for c in range(FC):
                    last = nc.tensor.matmul(h_ps[u % 2][:, c * P:(c + 1) * P], w1_now[u % 2][:, c * P:(c + 1) * P],
                                            toknT[u % 2][:], start=True, stop=True)
                last.then_inc(h_done, 1)

            def down(j, u, at):
                pe.wait_ge(gelu_done, nth(j))
                pe.wait_ge(y_added, nth(j - 2))
                for c in range(FC):
                    last = nc.tensor.matmul(y_ps[u % 2], hT[u % 2][:, c * P:(c + 1) * P],
                                            w2_sb[:, bass.ds(at + c * D, D)], start=(c == 0), stop=(c == FC - 1))
                last.then_inc(y_done, 1)

            pe.wait_ge(expert_w_in, 16 * 2 * E)
            pe.wait_ge(table_ready, 1)
            experts_of(0)
            transpose_tile(0, 0)
            transpose_tile(1, 1)
            up(0, 0)

            def tile(j, i, u):
                if not isinstance(j, int) or j + 2 < FFN_TILES:
                    transpose_tile(j + 2, u)
                if not isinstance(j, int) or j + 1 < FFN_TILES:
                    up(j + 1, u + 1)
                down(j, u, w_at[u])

            tiles(pe, tile, iteration=experts_of, last=lambda: experts_of(LOOPS))


_INS = ["x", "ctx_512", "g_xattn", "g_ffn", "L0_xattn_Wq", "L0_xattn_bq", "L0_xattn_Wk", "L0_xattn_bk",
        "L0_xattn_Wv", "L0_xattn_bv", "L0_ffn_Wr", "L0_ffn_br", "L0_ffn_W1", "L0_ffn_W2"]


def kernel(**inputs):
    import numpy as _np
    import concourse.bacc as _bacc
    from concourse import mybir as _mybir
    from concourse.bass_utils import run_bass_kernel_spmd as _run

    nc = _bacc.Bacc("TRN2", target_bir_lowering=False, num_devices=1)
    arrays, args = {}, []
    for name in _INS:
        a = _np.ascontiguousarray(inputs[name])
        arrays[f"in_{name}_dram"] = a
        args.append(nc.dram_tensor(f"in_{name}_dram", a.shape, _mybir.dt.from_np(a.dtype), kind="ExternalInput").ap())
    shape = _np.shape(inputs["x"])
    args.append(nc.dram_tensor("out_0_dram", shape, _mybir.dt.float32, kind="ExternalOutput").ap())
    attention_moe(nc, *args)
    r = _run(nc, [arrays], core_ids=[0])
    return r.results[0]["out_0_dram"]
```

```python
from contextlib import ExitStack

import concourse.bass as bass
from concourse import mybir

P = 128
F32 = mybir.dt.float32
BF16 = mybir.dt.bfloat16
I32 = mybir.dt.int32
ALU = mybir.AluOpType
ACT = mybir.ActivationFunctionType
AX = mybir.AxisListType

LN_EPS = 1e-5
GT = 4
CREDIT = 2
LEAD = 4
RING = 6

SHIFT, RSTD, SCALE, TOKEN, ROW = 128, 129, 130, 131, 132


def nth(g, last=None):
    if isinstance(g, int):
        g = max(g if last is None else min(g, last), -CREDIT)
    return g + 1 + CREDIT


def attention_moe(nc, x, ctx_in, g_xattn, g_ffn, Wq, bq, Wk, bk, Wv, bv, Wr, br, W1, W2, out):
    B, S, D = x.shape
    KD = ctx_in.shape[2]
    KA = KD + 1
    E, _, F = W1.shape
    N = B * S
    TILES = N // P
    NG = TILES // GT
    FC = F // P
    FFN_TILES = (N + E * (P - 1)) // P
    REGION = N + P
    SPARE = FFN_TILES - TILES
    TABLE = -(-(FFN_TILES + 1) // RING)
    TW = 8
    assert D == P and S == 64 and KD == 64 and GT * P == 512 and NG % 2 == 0 and NG > LEAD and F == 512
    assert (E - 1) * REGION // P < 256
    assert ROW == D + 4 and SPARE < E

    scratch = nc.dram_tensor("scratch", (E * REGION + SPARE * P, ROW), F32, kind="Internal").ap()

    x_tok = x.rearrange("b s d -> (b s) d").rearrange("(t p) d -> p t d", p=P)
    ctx_tok = ctx_in.rearrange("b s d -> (b s) d").rearrange("(t p) d -> p t d", p=P)
    out_tok = out.rearrange("b s d -> (b s) d")

    with ExitStack() as stack:
        def sb(name, shape, dt=F32):
            return stack.enter_context(nc.sbuf_tensor(name, shape, dt))

        def sem(name):
            return stack.enter_context(nc.semaphore(name))

        x_all = sb("x_all", [P, TILES * D])
        w1_sb = sb("w1_sb", [P, E * F])
        w2_sb = sb("w2_sb", [P, E * FC * D])
        wq_sb = sb("wq_sb", [P, D])
        wk_sb = sb("wk_sb", [KA, D])
        wv_sb = sb("wv_sb", [KA, D])
        wvg_sb = sb("wvg_sb", [KA, D + 1])
        bq_col = sb("bq_col", [P, 1])
        wr_sb = sb("wr_sb", [P, E])
        br_sb = sb("br_sb", [P, E])
        gates = sb("gates", [P, 2])
        tanh_gates = sb("tanh_gates", [P, 2])
        ident = sb("ident", [P, P])
        before = sb("before", [P, P], BF16)
        ones_b = sb("ones_b", [P, P], BF16)
        minus_half = sb("minus_half", [P, 2 * GT])
        first_row = sb("first_row", [P, P])
        region_part = sb("region_part", [P, GT, E], BF16)
        region_of = sb("region_of", [1, E])
        first_wins = sb("first_wins", [P, GT, E])
        wqT_sb = sb("wqT_sb", [P, D])
        wkT_sb = sb("wkT_sb", [P, KA])
        mv1 = sb("mv1", [P, TILES, 2])
        rows = sb("rows", [P, TILES, ROW])
        row_at = sb("row_at", [P, TILES], I32)
        wqk_sb = sb("wqk_sb", [P, KA])
        bqk_sb = sb("bqk_sb", [KA, 1])
        ctx_sb = [sb(f"ctx_{i}", [P, GT, KA]) for i in range(2)]
        stats1 = sb("stats1", [P, TILES, 6])
        stats2 = sb("stats2", [P, GT, 6])
        mv2 = [sb(f"mv2_{i}", [P, GT, 2]) for i in range(2)]
        xn = [sb(f"xn_{i}", [P, GT, D]) for i in range(2)]
        xnT = [sb(f"xnT_{i}", [P, GT * P]) for i in range(2)]
        ctxT = [sb(f"ctxT_{i}", [KA, GT * P]) for i in range(2)]
        qT = [sb(f"qT_{i}", [KA, GT * P]) for i in range(2)]
        rowmax = sb("rowmax", [P, GT])
        shifted = [sb(f"shifted_{i}", [P, GT, S]) for i in range(2)]
        probs = [sb(f"probs_{i}", [P, GT, P]) for i in range(2)]
        probsT = [sb(f"probsT_{i}", [P, GT * P]) for i in range(2)]
        mixT = [sb(f"mixT_{i}", [KA, GT * P]) for i in range(2)]
        inv_sum = sb("inv_sum", [P, 2, GT // 2, 1])
        x2n = [sb(f"x2n_{i}", [P, GT, D]) for i in range(2)]
        x2nT = [sb(f"x2nT_{i}", [P, GT * P]) for i in range(2)]
        exp_neg = sb("exp_neg", [P, GT, E])
        one_plus = sb("one_plus", [P, GT, E])
        least = sb("least", [P, GT, 1])
        route_max = [sb(f"route_max_{i}", [P, GT, 1]) for i in range(2)]
        is_max = sb("is_max", [P, GT, E])
        rank_max = sb("rank_max", [P, GT, E])
        best = sb("best", [P, GT, 1])
        onehot = [sb(f"onehot_{i}", [P, GT, E], BF16) for i in range(2)]
        group_sum = sb("group_sum", [P, E])
        so_far = [sb(f"so_far_{i}", [P, E], BF16) for i in range(2)]
        place_of = sb("place_of", [P, GT, E])
        pad_rows = sb("pad_rows", [P, ROW])
        multiples = sb("multiples", [1, E, TILES])
        tile_no = sb("tile_no", [1, TABLE * TW, E])
        tile_row = sb("tile_row", [1, TABLE * TW])
        ones_e = sb("ones_e", [1, E])
        counts = sb("counts", [1, E])
        pad_at = sb("pad_at", [1, E], I32)
        full = sb("full", [1, E, TILES])
        n_tiles = sb("n_tiles", [1, E])
        end_tile = sb("end_tile", [1, E])
        passed = sb("passed", [1, TABLE * TW, E])
        passed_tiles = sb("passed_tiles", [1, TABLE * TW, E])
        expert = sb("expert", [1, TABLE * TW])
        first_tile = sb("first_tile", [1, TABLE * TW])
        row_raw = sb("row_raw", [1, TABLE * TW])
        tile_at = sb("tile_at", [1, TABLE * TW], I32)
        weights_at = sb("weights_at", [1, TABLE * TW], I32)
        tok = [sb(f"tok_{i}", [P, ROW]) for i in range(RING)]
        tokn = [sb(f"tokn_{i}", [P, D]) for i in range(2)]
        toknT = [sb(f"toknT_{i}", [P, P]) for i in range(2)]
        w1_now = [sb(f"w1_now_{i}", [P, F]) for i in range(2)]
        hT = [sb(f"hT_{i}", [P, F]) for i in range(2)]

        bank_xT = stack.enter_context(nc.psum_tensor("bank_xT", [P, 512], F32))
        bank_ctx = stack.enter_context(nc.psum_tensor("bank_ctx", [P, 512], F32))
        bank_q = stack.enter_context(nc.psum_tensor("bank_q", [P, 512], F32))
        bank_s = stack.enter_context(nc.psum_tensor("bank_s", [P, 512], F32))
        bank_p = stack.enter_context(nc.psum_tensor("bank_p", [P, 512], F32))
        bank_m = stack.enter_context(nc.psum_tensor("bank_m", [P, 512], F32))
        banks_o = stack.enter_context(nc.psum_tensor("banks_o", [P, 2, 512], F32))
        s_ps = bank_s[:, 0:GT * S].rearrange("p (t k) -> p t k", t=GT)
        lg_ps = bank_ctx[:, 0:GT * E].rearrange("p (t e) -> p t e", t=GT)
        pf_ps = bank_ctx[:, GT * E:2 * GT * E].rearrange("p (t e) -> p t e", t=GT)
        cnt_ps = bank_ctx[:, 0:E]
        o_ps = banks_o[:, :, 0:2 * (D + 1)].rearrange("p b (t c) -> p b t c", c=D + 1)
        wT_ps, wkT_ps = bank_p[:, 0:D], bank_p[:, D:D + KA]
        wqk_ps, bqk_ps = bank_m[:, 0:KA], bank_m[0:KA, KA:KA + 1]
        tT_ps = [bank_xT[:, 0:P], bank_ctx[:, 0:P]]
        h_ps = [bank_q, bank_p]
        y_ps = [banks_o[:, 0, 0:D], banks_o[:, 1, 0:D]]

        x_in = [sem("x_in0"), sem("x_in1"), sem("x_in_rest")]
        ctx_in_sem = [sem("ctx_in0"), sem("ctx_in1")]
        attn_w_in, route_w_in, expert_w_in = sem("attn_w_in"), sem("route_w_in"), sem("expert_w_in")
        zeroed, consts_ready, ids_ready, table_consts = (
            sem("zeroed"), sem("consts_ready"), sem("ids_ready"), sem("table_consts"))
        gates_ready, wv_ready = sem("gates_ready"), sem("wv_ready")
        wT_ready, wT_copied, folded, folded_copied = (
            sem("wT_ready"), sem("wT_copied"), sem("folded"), sem("folded_copied"))
        def stages(*names):
            return [sem(n) for n in names]

        by_dve = xn_ready, shifted_ready, x2_ready, ln2_stats, onehot_ready, placed = stages(
            "xn_ready", "shifted_ready", "x2_ready", "ln2_stats", "onehot_ready", "placed")
        by_act = x2n_ready, xnT_copied, ctxT_copied, qT_copied, probs_ready, probsT_copied, mixT_copied, x2nT_copied, \
            exp_ready = stages("x2n_ready", "xnT_copied", "ctxT_copied", "qT_copied", "probs_ready", "probsT_copied",
                               "mixT_copied", "x2nT_copied", "exp_ready")
        by_pe = xnT_done, ctxT_done, qT_done, scores_done, probsT_done, mix_done, attn_done, x2nT_done, \
            logits_done, prefix_done = stages("xnT_done", "ctxT_done", "qT_done", "scores_done", "probsT_done",
                                              "mix_done", "attn_done", "x2nT_done", "logits_done", "prefix_done")
        by_pool = rstd2_ready, scale_ready = stages("rstd2_ready", "scale_ready")
        ln1_stats, rstd1_ready = sem("ln1_stats"), sem("rstd1_ready")
        scattered = sem("scattered")
        bn1, bn2, max_done, sums_done, routing = (
            sem("bn1"), sem("bn2"), sem("max_done"), sem("sums_done"), sem("routing"))
        ROUTING = 8
        eps1, eps2, pow2 = sem("eps1"), sem("eps2"), sem("pow2")
        wait_over, spare_written = sem("wait_over"), sem("spare_written")
        counts_done, counts_copied, pad_at_ready, table_step, table_ready, pads_written = (
            sem("counts_done"), sem("counts_copied"), sem("pad_at_ready"), sem("table_step"),
            sem("table_ready"), sem("pads_written"))
        pads_ready = sem("pads_ready")
        tok_in = [sem(f"tok_in{i}") for i in range(RING)]
        tok_out = [sem(f"tok_out{i}") for i in range(RING)]
        ffn_dve = tokn_ready, toknT_copied, y_added = stages("tokn_ready", "toknT_copied", "y_added")
        ffn_pe = toknT_done, h_done, y_done = stages("toknT_done", "h_done", "y_done")
        gelu_done, w1_copied = sem("gelu_done"), sem("w1_copied")

        def steps(eng, body):
            for k in range(LEAD):
                body(k, k // 2, k % 2)
            with eng.Fori(LEAD // 2, NG // 2) as i:
                for u in (0, 1):
                    body(i * 2 + u, i, u)
            for k in range(NG, NG + 3):
                body(k, k // 2, k % 2)

        def live(k, lag):
            return not isinstance(k, int) or 0 <= k - lag < NG

        LOOPS = FFN_TILES // RING

        def tiles(eng, body, iteration=None, last=None):
            with eng.Fori(0, LOOPS) as i:
                if iteration:
                    iteration(i)
                for u in range(RING):
                    body(i * RING + u, i, u)
            if last:
                last()
            for j in range(LOOPS * RING, FFN_TILES):
                body(j, LOOPS, j % RING)

        def give_credit(eng, sems):
            for s in sems:
                eng.sem_inc(s, CREDIT)

        def wait_apart(eng, s, count):
            eng.wait_ge(s, count)
            eng.sem_inc(wait_over, 1)

        block = stack.enter_context(nc.Block())

        @block.sync
        def _(sp):
            def load_x(g0, g1, which):
                sp.dma_start(x_all[:, g0 * GT * D:g1 * GT * D].rearrange("p (t d) -> p t d", d=D),
                             x_tok[:, g0 * GT:g1 * GT, :]).then_inc(x_in[which], 16)

            def load_ctx(g, p):
                sp.dma_start(ctx_sb[p][:, :, 0:KD], ctx_tok[:, bass.ds(g * GT, GT), :]).then_inc(ctx_in_sem[p], 16)

            def load_expert(e):
                sp.dma_start(w1_sb[:, bass.ds(e * F, F)], W1.rearrange("e p f -> p e f")[:, bass.ds(e, 1), :]
                             .rearrange("p a f -> p (a f)")).then_inc(expert_w_in, 16)
                sp.dma_start(w2_sb[:, bass.ds(e * F, F)].rearrange("p (c d) -> p c d", d=D),
                             W2.rearrange("e (c p) d -> p (e c) d", p=P)[:, bass.ds(e * FC, FC), :]
                             ).then_inc(expert_w_in, 16)

            load_x(0, 1, 0)
            load_x(1, 2, 1)
            sp.dma_start(wq_sb[:], Wq).then_inc(attn_w_in, 16)
            sp.dma_start(wk_sb[0:KD, :], Wk).then_inc(attn_w_in, 16)
            sp.dma_start(wk_sb[KD:KA, :], bk.rearrange("(a d) -> a d", a=1)).then_inc(attn_w_in, 16)
            sp.dma_start(wv_sb[0:KD, :], Wv).then_inc(attn_w_in, 16)
            sp.dma_start(wv_sb[KD:KA, :], bv.rearrange("(a d) -> a d", a=1)).then_inc(attn_w_in, 16)
            sp.dma_start(bq_col[:], bq.rearrange("(d a) -> d a", a=1)).then_inc(attn_w_in, 16)
            sp.dma_start(gates[:, 0:1], g_xattn.partition_broadcast(P)).then_inc(attn_w_in, 16)
            sp.dma_start(gates[:, 1:2], g_ffn.partition_broadcast(P)).then_inc(attn_w_in, 16)
            load_ctx(0, 0)
            load_x(2, NG, 2)
            load_ctx(1, 1)
            sp.dma_start(wr_sb[:], Wr).then_inc(route_w_in, 16)
            sp.dma_start(br_sb[:], br.partition_broadcast(P)).then_inc(route_w_in, 16)
            for e in range(E - NG + 2):
                load_expert(e)
            with sp.Fori(1, NG // 2) as i:
                for u in (0, 1):
                    g = i * 2 + u
                    sp.wait_ge(mix_done, nth(g - 2))
                    load_ctx(g, u)
                    load_expert(g + (E - NG))
            sp.wait_ge(pads_ready, 1)
            sp.dma_start(scratch[E * REGION:E * REGION + SPARE * P, :].rearrange("(t p) c -> p t c", p=P),
                         pad_rows[:].unsqueeze(1).broadcast_to([P, SPARE, ROW])).then_inc(spare_written, 16)

            sp.wait_ge(pad_at_ready, 1)
            regs = [sp.alloc_register(f"pad{e}") for e in range(E)]
            sp.reg_load(regs, pad_at[0:1, :])
            for e in range(E):
                at = sp.snap(regs[e], min_val=e * REGION, max_val=e * REGION + N)
                sp.dma_start(scratch[bass.ds(at, P), :], pad_rows[:]).then_inc(pads_written, 16)

            sp.wait_ge(table_ready, 1)
            sp.wait_ge(scattered, 16 * TILES)
            sp.wait_ge(spare_written, 16)
            sp.wait_ge(pads_written, 16 * E)
            at_regs = [sp.alloc_register(f"tile{m}") for m in range(RING)]

            def tile_rows(i, n):
                sp.reg_load(at_regs[0:n], tile_at[0:1, bass.ds(i * TW, n)])
                return [sp.snap(r, min_val=0, max_val=E * REGION + (SPARE - 1) * P) for r in at_regs[0:n]]

            def load_tile(at, u):
                sp.dma_start(tok[u][:], scratch[bass.ds(at, P), :]).then_inc(tok_in[u], 16)

            for u, at in enumerate(tile_rows(0, RING)):
                load_tile(at, u)
            with sp.Fori(1, LOOPS) as i:
                for u, at in enumerate(tile_rows(i, RING)):
                    sp.wait_ge(tok_out[u], i * 16)
                    load_tile(at, u)
            for u, at in enumerate(tile_rows(LOOPS, FFN_TILES - LOOPS * RING)):
                sp.wait_ge(tok_out[u], LOOPS * 16)
                load_tile(at, u)
            for u in range(RING):
                sp.wait_ge(tok_out[u], 16 * (LOOPS + (u < FFN_TILES - LOOPS * RING)))

        @block.gpsimd
        def _(pool):
            give_credit(pool, by_pool)
            nc.gpsimd.memset(ident[:], 0.0).then_inc(zeroed, 1)
            nc.gpsimd.memset(minus_half[:], -0.5)
            nc.gpsimd.memset(before[:], 0.0)
            nc.gpsimd.memset(first_row[:], 0.0).then_inc(zeroed, 1)
            pool.wait_ge(zeroed, 1)
            nc.gpsimd.affine_select(out=ident[:], in_=ident[:], compare_op=ALU.not_equal, fill=1.0, base=0,
                                    pattern=[[-1, P]], channel_multiplier=1)
            nc.gpsimd.memset(ctx_sb[0][:, :, KD:KA], 1.0)
            nc.gpsimd.memset(ctx_sb[1][:, :, KD:KA], 1.0).then_inc(consts_ready, 1)

            def rstd1(i):
                var = mv1[:, i * 2 * GT:(i + 1) * 2 * GT, 1:2]
                pool.wait_ge(ln1_stats, i + 1)
                nc.gpsimd.tensor_scalar(var, var, LN_EPS, None, ALU.add).then_inc(eps1, 1)
                pool.wait_ge(eps1, i + 1)
                nc.gpsimd.tensor_tensor(var, var, minus_half[:].unsqueeze(2), ALU.pow).then_inc(rstd1_ready, 1)

            rstd1(0)
            nc.gpsimd.memset(probs[0][:], 0.0)
            nc.gpsimd.memset(probs[1][:], 0.0).then_inc(consts_ready, 1)
            rstd1(1)
            pool.wait_ge(zeroed, 2)
            nc.gpsimd.affine_select(out=before[:], in_=before[:], compare_op=ALU.is_ge, fill=1.0, base=0,
                                    pattern=[[-1, P]], channel_multiplier=1)
            nc.gpsimd.affine_select(out=first_row[:], in_=first_row[:], compare_op=ALU.not_equal, fill=1.0, base=0,
                                    pattern=[[0, P]], channel_multiplier=1)
            nc.gpsimd.memset(ones_b[:], 1.0)
            nc.gpsimd.memset(so_far[0][:], 0.0)
            nc.gpsimd.iota(region_part[:], [[0, GT], [REGION // P, E]], base=0, channel_multiplier=0,
                           allow_small_or_imprecise_dtypes=True)
            nc.gpsimd.iota(first_wins[:], [[0, GT], [-1, E]], base=E, channel_multiplier=0,
                           allow_small_or_imprecise_dtypes=True).then_inc(consts_ready, 1)
            rstd1(2)
            nc.gpsimd.iota(rows[:, :, TOKEN:ROW].bitcast(I32), [[P, TILES]], base=0, channel_multiplier=1
                           ).then_inc(ids_ready, 1)
            nc.gpsimd.memset(pad_rows[:, 0:TOKEN], 0.0)
            nc.gpsimd.iota(pad_rows[:, TOKEN:ROW].bitcast(I32), [[0, 1]], base=N,
                           channel_multiplier=0).then_inc(pads_ready, 1)
            rstd1(3)
            nc.gpsimd.iota(multiples[:], [[0, E], [P, TILES]], base=0, channel_multiplier=0,
                           allow_small_or_imprecise_dtypes=True)
            nc.gpsimd.iota(tile_no[:], [[RING, TABLE], [1, TW], [0, E]], base=0, channel_multiplier=0,
                           allow_small_or_imprecise_dtypes=True)
            nc.gpsimd.iota(tile_row[:], [[RING * P, TABLE], [P, TW]], base=0, channel_multiplier=0,
                           allow_small_or_imprecise_dtypes=True)
            nc.gpsimd.iota(region_of[:], [[REGION, E]], base=0, channel_multiplier=0,
                           allow_small_or_imprecise_dtypes=True)
            nc.gpsimd.memset(ones_e[:], 1.0).then_inc(table_consts, 1)

            def norm2(g):
                mean, var = mv2[g % 2][:, :, 0:1], mv2[g % 2][:, :, 1:2]
                rstd = rows[:, g * GT:(g + 1) * GT, RSTD:SCALE]
                pool.wait_ge(ln2_stats, nth(g))
                nc.gpsimd.tensor_scalar(var, var, LN_EPS, None, ALU.add).then_inc(eps2, 1)
                nc.gpsimd.tensor_scalar(mean, mean, -1.0, None, ALU.mult)
                pool.wait_ge(eps2, g + 1)
                nc.gpsimd.tensor_tensor(rstd, var, minus_half[:, 0:GT].unsqueeze(2), ALU.pow).then_inc(pow2, 1)
                pool.wait_ge(pow2, g + 1)
                nc.gpsimd.tensor_tensor(rows[:, g * GT:(g + 1) * GT, SHIFT:RSTD], mean, rstd,
                                        ALU.mult).then_inc(rstd2_ready, 1)

            def scatter_rows(g):
                pool.wait_ge(placed, nth(g))
                nc.gpsimd.tensor_scalar(rows[:, g * GT:(g + 1) * GT, SCALE:TOKEN], route_max[g % 2][:],
                                        tanh_gates[:, 1:2], None, ALU.mult).then_inc(scale_ready, 1)
                pool.wait_ge(scale_ready, nth(g))
                for t in range(g * GT, (g + 1) * GT):
                    nc.gpsimd.indirect_dma_start(
                        out=scratch, out_offset=bass.IndirectOffsetOnAxis(ap=row_at[:, t:t + 1], axis=0),
                        in_=rows[:, t, :], in_offset=None).then_inc(scattered, 16)

            pool.wait_ge(ids_ready, 1)
            pool.wait_ge(gates_ready, 1)
            for g in range(NG + 1):
                if g < NG:
                    norm2(g)
                if g >= 1:
                    pool.wait_ge(rstd2_ready, nth(g - 1))
                    scatter_rows(g - 1)

            def scatter_tile(j, i, u):
                wait_apart(pool, y_added, nth(j))
                nc.gpsimd.indirect_dma_start(
                    out=out_tok, out_offset=bass.IndirectOffsetOnAxis(ap=tok[u][:, TOKEN:ROW].bitcast(I32), axis=0),
                    in_=tok[u][:, 0:D], in_offset=None, bounds_check=N - 1, oob_is_err=False).then_inc(tok_out[u], 16)

            tiles(pool, scatter_tile)

        @block.scalar
        def _(act):
            give_credit(act, by_act)
            act.sem_inc(gelu_done, CREDIT)
            act.wait_ge(attn_w_in, 16 * 8)
            nc.scalar.activation(tanh_gates[:], gates[:], ACT.Tanh).then_inc(gates_ready, 1)

            def body(k, i, u):
                def evacuate(dst, src, filled, freed, copied, g):
                    act.wait_ge(filled, nth(g))
                    act.wait_ge(freed, nth(g - 2))
                    nc.scalar.copy(dst, src).then_inc(copied, 1)

                v = 1 - u
                if live(k, 3):
                    act.wait_ge(rstd2_ready, nth(k - 3))
                    act.wait_ge(x2nT_done, nth(k - 5))
                    for t in range(GT):
                        def row(a, b):
                            return rows[:].rearrange("p t c -> p (t c)")[
                                :, bass.ds((k - 3) * (GT * ROW) + (t * ROW + a), b - a)]

                        last = nc.scalar.activation(x2n[v][:, t, :], row(0, D), ACT.Identity,
                                                    bias=row(SHIFT, RSTD), scale=row(RSTD, SCALE))
                    last.then_inc(x2n_ready, 1)
                if live(k, 1):
                    act.wait_ge(shifted_ready, nth(k - 1))
                    act.wait_ge(probsT_done, nth(k - 3))
                    nc.scalar.activation(probs[v][0:S, :, 0:S], shifted[v][0:S], ACT.Exp)
                    nc.scalar.activation(probs[v][S:P, :, S:P], shifted[v][S:P], ACT.Exp).then_inc(probs_ready, 1)
                if live(k, 0):
                    evacuate(ctxT[u][:], bank_ctx[0:KA, :], ctxT_done, scores_done, ctxT_copied, k)
                if live(k, 3):
                    evacuate(x2nT[v][:], bank_xT[:], x2nT_done, logits_done, x2nT_copied, k - 3)
                if live(k, 1):
                    evacuate(probsT[v][:], bank_p[:], probsT_done, mix_done, probsT_copied, k - 1)
                if live(k, 0):
                    evacuate(xnT[u][:], bank_xT[:], xnT_done, qT_done, xnT_copied, k)
                if live(k, 3):
                    act.wait_ge(logits_done, nth(k - 3))
                    act.wait_ge(onehot_ready, nth(k - 4))
                    nc.scalar.activation(exp_neg[:], lg_ps, ACT.Exp, scale=-1.0).then_inc(exp_ready, 1)
                if live(k, 1):
                    evacuate(mixT[v][:], bank_m[0:KA, :], mix_done, attn_done, mixT_copied, k - 1)
                if live(k, 0):
                    act.wait_ge(qT_done, nth(k))
                    act.wait_ge(scores_done, nth(k - 2))
                    nc.scalar.activation(qT[u][:], bank_q[0:KA, :], ACT.Identity,
                                         bias=bqk_sb[:, 0:1]).then_inc(qT_copied, 1)

            act.wait_ge(folded_copied, 2)
            steps(act, body)

            def gelu(j, i, u):
                act.wait_ge(h_done, nth(j))
                act.wait_ge(y_done, nth(j - 2))
                nc.scalar.activation(hT[u % 2][:], h_ps[u % 2][:], ACT.Gelu).then_inc(gelu_done, 1)

            tiles(act, gelu)

        @block.vector
        def _(dve):
            give_credit(dve, by_dve)
            give_credit(dve, ffn_dve)

            def fold_weights():
                dve.wait_ge(attn_w_in, 16 * 8)
                dve.wait_ge(gates_ready, 1)
                nc.vector.tensor_scalar(wvg_sb[:, 0:D], wv_sb[:], tanh_gates[0:KA, 0:1], None, ALU.mult)
                nc.vector.memset(wvg_sb[0:KD, D:D + 1], 0.0)
                nc.vector.memset(wvg_sb[KD:KA, D:D + 1], 1.0).then_inc(wv_ready, 1)
                dve.wait_ge(wT_ready, 1)
                nc.vector.tensor_copy(wqT_sb[:], wT_ps)
                nc.vector.tensor_copy(wkT_sb[:], wkT_ps).then_inc(wT_copied, 1)
                dve.wait_ge(folded, 1)
                nc.vector.tensor_copy(wqk_sb[:], wqk_ps).then_inc(folded_copied, 1)
                nc.vector.tensor_copy(bqk_sb[:], bqk_ps).then_inc(folded_copied, 1)

            def x_of(g, t):
                return x_all[:, bass.ds(g * (GT * D) + t * D, D)]

            def layer_stats1(i):
                for a in (0, 1) if i == 0 else (2,):
                    dve.wait_ge(x_in[a], 16)
                for t in range(2 * GT):
                    last = nc.vector.bn_stats(stats1[:, i * 2 * GT + t, :], x_of(i * 2, t))
                last.then_inc(bn1, 1)
                dve.wait_ge(bn1, i + 1)
                for t in range(2 * GT):
                    last = nc.vector.bn_aggr(mv1[:, i * 2 * GT + t, :], stats1[:, i * 2 * GT + t, :])
                last.then_inc(ln1_stats, 1)

            def normalise1(g, p):
                dve.wait_ge(rstd1_ready, g // 2 + 1 if isinstance(g, int) else NG // 2)
                dve.wait_ge(xnT_done, nth(g - 2))
                mv_flat = mv1[:].rearrange("p t c -> p (t c)")
                for t in range(GT):
                    def stat(c):
                        return mv_flat[:, bass.ds(g * (GT * 2) + (t * 2 + c), 1)]

                    last = nc.vector.tensor_scalar(xn[p][:, t, :], x_of(g, t), stat(0), stat(1),
                                                   ALU.subtract, ALU.mult)
                last.then_inc(xn_ready, 1)

            def softmax_shift(g, p):
                dve.wait_ge(scores_done, nth(g))
                nc.vector.tensor_reduce(rowmax[:], s_ps, AX.X, ALU.max).then_inc(max_done, 1)
                dve.wait_ge(max_done, g + 1)
                dve.wait_ge(probs_ready, nth(g - 2))
                nc.vector.tensor_tensor(shifted[p][:], s_ps, rowmax[:].unsqueeze(2).broadcast_to([P, GT, S]),
                                        ALU.subtract).then_inc(shifted_ready, 1)

            def residual1(g, p):
                def x2_of(t):
                    return rows[:].rearrange("p t c -> p (t c)")[:, bass.ds(g * (GT * ROW) + t * ROW, D)]

                dve.wait_ge(attn_done, nth(g))
                nc.vector.reciprocal(inv_sum[:], o_ps[:, :, :, D:D + 1]).then_inc(sums_done, 1)
                dve.wait_ge(sums_done, g + 1)
                for t in range(GT):
                    last = nc.vector.scalar_tensor_tensor(
                        out=x2_of(t), in0=o_ps[:, t // 2, t % 2, 0:D],
                        scalar=inv_sum[:, t // 2, t % 2, :], in1=x_of(g, t), op0=ALU.mult, op1=ALU.add)
                last.then_inc(x2_ready, 1)
                wait_apart(dve, x2_ready, nth(g))
                for t in range(GT):
                    last = nc.vector.bn_stats(stats2[:, t, :], x2_of(t))
                last.then_inc(bn2, 1)
                wait_apart(dve, bn2, g + 1)
                wait_apart(dve, rstd2_ready, nth(g - 2))
                for t in range(GT):
                    last = nc.vector.bn_aggr(mv2[p][:, t, :], stats2[:, t, :])
                last.then_inc(ln2_stats, 1)

            def choose(g, p):
                def link(ins, n):
                    ins.then_inc(routing, 1)
                    dve.wait_ge(routing, g * ROUTING + n)

                wide = [P, GT, E]
                dve.wait_ge(exp_ready, nth(g))
                link(nc.vector.tensor_scalar(one_plus[:], exp_neg[:], 1.0, None, ALU.add), 1)
                link(nc.vector.tensor_reduce(least[:], one_plus[:], AX.X, ALU.min), 2)
                link(nc.vector.tensor_tensor(is_max[:], one_plus[:], least[:].broadcast_to(wide), ALU.is_equal), 3)
                link(nc.vector.tensor_tensor(rank_max[:], is_max[:], first_wins[:], ALU.mult), 4)
                link(nc.vector.tensor_reduce(best[:], rank_max[:], AX.X, ALU.max), 5)
                dve.wait_ge(prefix_done, nth(g - 1))
                link(nc.vector.tensor_tensor(onehot[p][:], rank_max[:], best[:].broadcast_to(wide), ALU.is_equal), 6)
                link(nc.vector.tensor_reduce(group_sum[:], onehot[p][:].rearrange("p t e -> p e t"), AX.X, ALU.add), 7)
                nc.vector.tensor_tensor(so_far[1 - p][:], so_far[p][:], group_sum[:], ALU.add).then_inc(onehot_ready, 1)
                dve.wait_ge(scale_ready, nth(g - 2))
                nc.vector.reciprocal(route_max[p][:], least[:])

            def place_rows(g, p):
                dve.wait_ge(prefix_done, nth(g))
                nc.vector.tensor_tensor(place_of[:], pf_ps, onehot[p][:], ALU.mult).then_inc(routing, 1)
                dve.wait_ge(routing, g * ROUTING + 8)
                with nc.allow_low_precision(reason="whole numbers below 2**24 are exact"):
                    nc.vector.tensor_reduce(row_at[:, bass.ds(g * GT, GT)], place_of[:], AX.X, ALU.add
                                            ).then_inc(placed, 1)

            def body(k, i, u):
                v = 1 - u
                if live(k, 1):
                    softmax_shift(k - 1, v)
                if live(k, 0):
                    normalise1(k, u)
                if isinstance(k, int) and k + 2 < NG // 2:
                    layer_stats1(k + 2)
                if live(k, 2):
                    residual1(k - 2, u)
                if live(k, 3):
                    choose(k - 3, v)
                    place_rows(k - 3, v)

            layer_stats1(0)
            layer_stats1(1)
            fold_weights()
            dve.wait_ge(consts_ready, 3)
            steps(dve, body)

            table = [0]

            def link(ins):
                table[0] += 1
                ins.then_inc(table_step, 1)
                dve.wait_ge(table_step, table[0])

            deep = [1, TABLE * TW, E]
            dve.wait_ge(table_consts, 1)
            dve.wait_ge(counts_done, 1)
            link(nc.vector.tensor_copy(counts[:], cnt_ps[0:1, :]))
            nc.vector.tensor_tensor(pad_at[:], counts[:], region_of[:], ALU.add).then_inc(pad_at_ready, 1)
            link(nc.vector.tensor_tensor(full[:], counts[:].unsqueeze(2).broadcast_to([1, E, TILES]), multiples[:],
                                         ALU.is_gt))
            link(nc.vector.tensor_reduce(n_tiles[:], full[:], AX.X, ALU.add))
            link(nc.vector.tensor_tensor_scan(end_tile[:], ones_e[:], n_tiles[:], 0.0, ALU.mult, ALU.add))
            link(nc.vector.tensor_tensor(passed[:], end_tile[:].unsqueeze(1).broadcast_to(deep), tile_no[:], ALU.is_le))
            link(nc.vector.tensor_reduce(expert[:], passed[:], AX.X, ALU.add))
            link(nc.vector.tensor_tensor(passed_tiles[:], passed[:], n_tiles[:].unsqueeze(1).broadcast_to(deep), ALU.mult))
            link(nc.vector.tensor_reduce(first_tile[:], passed_tiles[:], AX.X, ALU.add))
            nc.vector.tensor_scalar(weights_at[:], expert[:], float(E - 1), float(F), ALU.min, ALU.mult)
            link(nc.vector.scalar_tensor_tensor(out=row_raw[:], in0=expert[:], scalar=float(REGION), in1=tile_row[:],
                                                op0=ALU.mult, op1=ALU.add))
            nc.vector.scalar_tensor_tensor(out=tile_at[:], in0=first_tile[:], scalar=float(-P), in1=row_raw[:],
                                           op0=ALU.mult, op1=ALU.add).then_inc(table_ready, 1)

            def normalise_tile(j, i, u):
                dve.wait_ge(tok_in[u], i * 16 + 16)
                dve.wait_ge(toknT_done, nth(j - 2))
                nc.vector.tensor_scalar(tokn[u % 2][:], tok[u][:, 0:D], tok[u][:, RSTD:SCALE], tok[u][:, SHIFT:RSTD],
                                        ALU.mult, ALU.add).then_inc(tokn_ready, 1)

            def copy_transposed(j, u):
                dve.wait_ge(toknT_done, nth(j))
                dve.wait_ge(h_done, nth(j - 2))
                nc.vector.tensor_copy(toknT[u % 2][:], tT_ps[u % 2]).then_inc(toknT_copied, 1)

            def copy_w1(u, at):
                nc.vector.tensor_copy(w1_now[u % 2][:], w1_sb[:, bass.ds(at, F)]).then_inc(w1_copied, 1)

            def residual2(j, u):
                dve.wait_ge(y_done, nth(j))
                nc.vector.scalar_tensor_tensor(out=tok[u][:, 0:D], in0=y_ps[u % 2], scalar=tok[u][:, SCALE:TOKEN],
                                               in1=tok[u][:, 0:D], op0=ALU.mult, op1=ALU.add).then_inc(y_added, 1)

            w_regs = [dve.alloc_register(f"wd{m}") for m in range(TW)]
            w_at = []

            def experts_of(i):
                dve.reg_load(w_regs, weights_at[0:1, bass.ds(i * TW, TW)])
                w_at[:] = [dve.snap(r, min_val=0, max_val=(E - 1) * F) for r in w_regs]

            dve.wait_ge(table_ready, 1)
            dve.wait_ge(expert_w_in, 16 * 2 * E)
            experts_of(0)
            copy_w1(0, w_at[0])
            copy_w1(1, w_at[1])
            normalise_tile(0, 0, 0)
            normalise_tile(1, 0, 1)
            copy_transposed(0, 0)
            copy_transposed(1, 1)
            normalise_tile(2, 0, 2)

            def tile(j, i, u):
                if not isinstance(j, int) or j + 2 < FFN_TILES:
                    copy_transposed(j + 2, u + 2)
                    copy_w1(u + 2, w_at[u + 2])
                if not isinstance(j, int) or j + 3 < FFN_TILES:
                    normalise_tile(j + 3, i + (u + 3) // RING, (u + 3) % RING)
                residual2(j, u)

            tiles(dve, tile, iteration=experts_of, last=lambda: experts_of(LOOPS))

        @block.tensor
        def _(pe):
            give_credit(pe, by_pe)
            give_credit(pe, ffn_pe)
            pe.wait_ge(consts_ready, 1)
            pe.wait_ge(attn_w_in, 16 * 8)
            nc.tensor.transpose(wT_ps, wq_sb[:], ident[:])
            nc.tensor.transpose(wkT_ps, wk_sb[:], ident[0:KA, 0:KA]).then_inc(wT_ready, 1)
            pe.wait_ge(wT_copied, 1)
            nc.tensor.matmul(wqk_ps, wqT_sb[:], wkT_sb[:], start=True, stop=True)
            nc.tensor.matmul(bqk_ps, wkT_sb[:], bq_col[:], start=True, stop=True).then_inc(folded, 1)
            pe.wait_ge(folded_copied, 2)
            pe.wait_ge(wv_ready, 1)

            def transposes(dst, src, done):
                for t in range(GT):
                    last = nc.tensor.transpose(dst[:, t * P:(t + 1) * P], src[:, t, :], ident[:])
                last.then_inc(done, 1)

            def scores(g, p):
                pe.wait_ge(qT_copied, nth(g))
                pe.wait_ge(ctxT_copied, nth(g))
                pe.wait_ge(shifted_ready, nth(g - 1))
                for t in range(GT):
                    for b in range(2):
                        cols = slice(t * P + b * S, t * P + b * S + S)
                        last = nc.tensor.matmul(s_ps[b * S:b * S + S, t, :], qT[p][:, cols], ctxT[p][:, cols],
                                                start=True, stop=True)
                last.then_inc(scores_done, 1)

            def prefix(g, p):
                pe.wait_ge(onehot_ready, nth(g))
                nc.tensor.matmul(pf_ps, before[:], onehot[p][:], start=True, stop=False)
                for t in range(GT - 1):
                    nc.tensor.matmul(pf_ps[:, t + 1:GT, :], ones_b[:],
                                     onehot[p][:, t:t + 1, :].broadcast_to([P, GT - 1 - t, E]),
                                     start=False, stop=False)
                nc.tensor.matmul(pf_ps, ones_b[:], region_part[:], start=False, stop=False)
                nc.tensor.matmul(pf_ps, ones_b[:], so_far[p][:].unsqueeze(1).broadcast_to([P, GT, E]),
                                 start=False, stop=True).then_inc(prefix_done, 1)

            def body(k, i, u):
                v = 1 - u
                if live(k, 0):
                    pe.wait_ge(ctx_in_sem[u], i * 16 + 16)
                    pe.wait_ge(placed, nth(k - 4))
                    transposes(bank_ctx[0:KA, :], ctx_sb[u], ctxT_done)
                if live(k, 3):
                    pe.wait_ge(x2n_ready, nth(k - 3))
                    pe.wait_ge(xnT_copied, nth(k - 1, NG - 1))
                    transposes(bank_xT, x2n[v], x2nT_done)
                if live(k, 1):
                    pe.wait_ge(probs_ready, nth(k - 1))
                    pe.wait_ge(probsT_copied, nth(k - 2))
                    transposes(bank_p, probs[v], probsT_done)
                if live(k, 0):
                    pe.wait_ge(xn_ready, nth(k))
                    pe.wait_ge(x2nT_copied, nth(k - 3))
                    transposes(bank_xT, xn[u], xnT_done)
                if live(k, 3):
                    pe.wait_ge(x2nT_copied, nth(k - 3))
                    pe.wait_ge(placed, nth(k - 4))
                    pe.wait_ge(ctxT_copied, nth(k, NG - 1))
                    nc.tensor.matmul(lg_ps, first_row[:], br_sb[:].unsqueeze(1).broadcast_to([P, GT, E]),
                                     start=True, stop=False)
                    for t in range(GT):
                        last = nc.tensor.matmul(lg_ps[:, t, :], x2nT[v][:, t * P:(t + 1) * P], wr_sb[:],
                                                start=False, stop=(t == GT - 1))
                    last.then_inc(logits_done, 1)
                if live(k, 1):
                    pe.wait_ge(probsT_copied, nth(k - 1))
                    pe.wait_ge(mixT_copied, nth(k - 2))
                    for t in range(GT):
                        last = nc.tensor.matmul(bank_m[0:KA, t * P:(t + 1) * P], ctx_sb[v][:, t, :],
                                                probsT[v][:, t * P:(t + 1) * P], start=True, stop=True)
                    last.then_inc(mix_done, 1)
                if live(k, 0):
                    pe.wait_ge(xnT_copied, nth(k))
                    pe.wait_ge(qT_copied, nth(k - 1))
                    nc.tensor.matmul(bank_q[0:KA, :], wqk_sb[:], xnT[u][:], start=True, stop=True).then_inc(qT_done, 1)
                if live(k, 1):
                    pe.wait_ge(mixT_copied, nth(k - 1))
                    pe.wait_ge(x2_ready, nth(k - 2))
                    for t in range(GT):
                        last = nc.tensor.matmul(o_ps[:, t // 2, t % 2, :], mixT[v][:, t * P:(t + 1) * P], wvg_sb[:],
                                                start=True, stop=True)
                    last.then_inc(attn_done, 1)
                if live(k, 0):
                    scores(k, u)
                if live(k, 3):
                    prefix(k - 3, v)

            pe.wait_ge(consts_ready, 3)
            pe.wait_ge(route_w_in, 32)
            steps(pe, body)

            pe.wait_ge(placed, nth(NG - 1))
            nc.tensor.matmul(cnt_ps, ones_b[:], so_far[NG % 2][:], start=True, stop=True).then_inc(counts_done, 1)

            w_regs = [pe.alloc_register(f"w{m}") for m in range(RING)]
            w_at = []

            def experts_of(i):
                pe.reg_load(w_regs, weights_at[0:1, bass.ds(i * TW, RING)])
                w_at[:] = [pe.snap(r, min_val=0, max_val=(E - 1) * F) for r in w_regs]

            def transpose_tile(j, u):
                pe.wait_ge(tokn_ready, nth(j))
                pe.wait_ge(toknT_copied, nth(j - 2))
                nc.tensor.transpose(tT_ps[u % 2], tokn[u % 2][:], ident[:]).then_inc(toknT_done, 1)

            def up(j, u):
                pe.wait_ge(toknT_copied, nth(j))
                pe.wait_ge(w1_copied, j + 1)
                pe.wait_ge(gelu_done, nth(j - 2))
                for c in range(FC):
                    last = nc.tensor.matmul(h_ps[u % 2][:, c * P:(c + 1) * P], w1_now[u % 2][:, c * P:(c + 1) * P],
                                            toknT[u % 2][:], start=True, stop=True)
                last.then_inc(h_done, 1)

            def down(j, u, at):
                pe.wait_ge(gelu_done, nth(j))
                pe.wait_ge(y_added, nth(j - 2))
                for c in range(FC):
                    last = nc.tensor.matmul(y_ps[u % 2], hT[u % 2][:, c * P:(c + 1) * P],
                                            w2_sb[:, bass.ds(at + c * D, D)], start=(c == 0), stop=(c == FC - 1))
                last.then_inc(y_done, 1)

            pe.wait_ge(expert_w_in, 16 * 2 * E)
            pe.wait_ge(table_ready, 1)
            experts_of(0)
            transpose_tile(0, 0)
            transpose_tile(1, 1)
            up(0, 0)

            def tile(j, i, u):
                if not isinstance(j, int) or j + 2 < FFN_TILES:
                    transpose_tile(j + 2, u)
                if not isinstance(j, int) or j + 1 < FFN_TILES:
                    up(j + 1, u + 1)
                down(j, u, w_at[u])

            tiles(pe, tile, iteration=experts_of, last=lambda: experts_of(LOOPS))


_INS = ["x", "ctx_512", "g_xattn", "g_ffn", "L0_xattn_Wq", "L0_xattn_bq", "L0_xattn_Wk", "L0_xattn_bk",
        "L0_xattn_Wv", "L0_xattn_bv", "L0_ffn_Wr", "L0_ffn_br", "L0_ffn_W1", "L0_ffn_W2"]


def kernel(**inputs):
    import numpy as _np
    import concourse.bacc as _bacc
    from concourse import mybir as _mybir
    from concourse.bass_utils import run_bass_kernel_spmd as _run

    nc = _bacc.Bacc("TRN2", target_bir_lowering=False, num_devices=1)
    arrays, args = {}, []
    for name in _INS:
        a = _np.ascontiguousarray(inputs[name])
        arrays[f"in_{name}_dram"] = a
        args.append(nc.dram_tensor(f"in_{name}_dram", a.shape, _mybir.dt.from_np(a.dtype), kind="ExternalInput").ap())
    shape = _np.shape(inputs["x"])
    args.append(nc.dram_tensor("out_0_dram", shape, _mybir.dt.float32, kind="ExternalOutput").ap())
    attention_moe(nc, *args)
    r = _run(nc, [arrays], core_ids=[0])
    return r.results[0]["out_0_dram"]
```

```python
from contextlib import ExitStack

import concourse.bass as bass
from concourse import mybir

P = 128
F32 = mybir.dt.float32
BF16 = mybir.dt.bfloat16
I32 = mybir.dt.int32
ALU = mybir.AluOpType
ACT = mybir.ActivationFunctionType
AX = mybir.AxisListType

LN_EPS = 1e-5
GT = 4
CREDIT = 2
LEAD = 4
RING = 6

MEAN, RSTD, SCALE, TOKEN, ROW = 128, 129, 130, 131, 132


def nth(g, last=None):
    if isinstance(g, int):
        g = max(g if last is None else min(g, last), -CREDIT)
    return g + 1 + CREDIT


def attention_moe(nc, x, ctx_in, g_xattn, g_ffn, Wq, bq, Wk, bk, Wv, bv, Wr, br, W1, W2, out):
    B, S, D = x.shape
    KD = ctx_in.shape[2]
    KA = KD + 1
    E, _, F = W1.shape
    N = B * S
    TILES = N // P
    NG = TILES // GT
    FC = F // P
    FFN_TILES = (N + E * (P - 1)) // P
    REGION = N + P
    SPARE = FFN_TILES - TILES
    STATS1 = [(0, 1), (1, 2)] + [(g, g + 2) for g in range(2, NG, 2)]
    LOOPS = FFN_TILES // RING
    TW = RING + 2
    TABLE = LOOPS * RING + TW
    FIRST_GROUPS, FIRST_LOOPS = NG - 3, 2
    FIRST_TILES = FIRST_LOOPS * RING
    LATER = TABLE - FIRST_TILES
    assert FIRST_GROUPS * GT * P - E * (P - 1) > (FIRST_TILES - 1) * P
    assert D == P and S == 64 and KD == 64 and GT * P == 512 and NG % 2 == 0 and NG > LEAD and F == 512
    assert (E - 1) * REGION // P < 256
    assert ROW == D + 4 and SPARE < E

    scratch = nc.dram_tensor("scratch", (E * REGION + SPARE * P, ROW), F32, kind="Internal").ap()

    x_tok = x.rearrange("b s d -> (b s) d").rearrange("(t p) d -> p t d", p=P)
    ctx_tok = ctx_in.rearrange("b s d -> (b s) d").rearrange("(t p) d -> p t d", p=P)
    out_tok = out.rearrange("b s d -> (b s) d")

    with ExitStack() as stack:
        def sb(name, shape, dt=F32):
            return stack.enter_context(nc.sbuf_tensor(name, shape, dt))

        def sem(name):
            return stack.enter_context(nc.semaphore(name))

        x_all = sb("x_all", [P, TILES * D])
        w1_sb = sb("w1_sb", [P, E * F])
        w2_sb = sb("w2_sb", [P, E * FC * D])
        wq_sb = sb("wq_sb", [P, D])
        wk_sb = sb("wk_sb", [KA, D])
        wv_sb = sb("wv_sb", [KA, D])
        wvg_sb = sb("wvg_sb", [KA, D + 1])
        bq_col = sb("bq_col", [P, 1])
        wr_sb = sb("wr_sb", [P, E])
        br_sb = sb("br_sb", [P, E])
        gates = sb("gates", [P, 2])
        tanh_gates = sb("tanh_gates", [P, 2])
        gelu_table = sb("gelu_table", [P, 2])
        ident = sb("ident", [P, P])
        before = sb("before", [P, P], BF16)
        ones_b = sb("ones_b", [P, P], BF16)
        minus_half = sb("minus_half", [P, 2 * GT])
        averaging = sb("averaging", [P, P])
        region_part = sb("region_part", [P, GT, E], BF16)
        region_of = sb("region_of", [1, E])
        first_wins = sb("first_wins", [P, GT, E])
        wqT_sb = sb("wqT_sb", [P, D])
        wkT_sb = sb("wkT_sb", [P, KA])
        mv1 = sb("mv1", [P, TILES, 2])
        rows = sb("rows", [P, TILES, ROW])
        row_at = sb("row_at", [P, TILES], I32)
        wr_centred = sb("wr_centred", [P, E])
        wqk_sb = sb("wqk_sb", [P, KA])
        bqk_sb = sb("bqk_sb", [KA, 1])
        ctx_sb = [sb(f"ctx_{i}", [P, GT, KA]) for i in range(2)]
        stats1 = sb("stats1", [P, TILES, 6])
        stats2 = sb("stats2", [P, GT, 6])
        mv2 = [sb(f"mv2_{i}", [P, GT, 2]) for i in range(2)]
        xn = [sb(f"xn_{i}", [P, GT, D]) for i in range(2)]
        xnT = [sb(f"xnT_{i}", [P, GT * P]) for i in range(2)]
        ctxT = [sb(f"ctxT_{i}", [KA, GT * P]) for i in range(2)]
        qT = [sb(f"qT_{i}", [KA, GT * P]) for i in range(2)]
        rowmax = sb("rowmax", [P, GT])
        shifted = [sb(f"shifted_{i}", [P, GT, S]) for i in range(2)]
        probs = [sb(f"probs_{i}", [P, GT, P]) for i in range(2)]
        probsT = [sb(f"probsT_{i}", [P, GT * P]) for i in range(2)]
        mixT = [sb(f"mixT_{i}", [KA, GT * P]) for i in range(2)]
        inv_sum = sb("inv_sum", [P, 2, GT // 2, 1])
        x2 = [sb(f"x2_{i}", [P, GT, D]) for i in range(2)]
        x2T = [sb(f"x2T_{i}", [P, GT * P]) for i in range(2)]
        scaled = sb("scaled", [P, GT, E])
        logits = sb("logits", [P, GT, E])
        exp_neg = sb("exp_neg", [P, GT, E])
        exp_neg_last = sb("exp_neg_last", [P, GT, E])
        one_plus = sb("one_plus", [P, GT, E])
        least = sb("least", [P, GT, 1])
        route_max = sb("route_max", [P, GT, 1])
        is_max = sb("is_max", [P, GT, E])
        rank_max = sb("rank_max", [P, GT, E])
        best = sb("best", [P, GT, 1])
        onehot = [sb(f"onehot_{i}", [P, GT, E], BF16) for i in range(2)]
        group_sum = sb("group_sum", [P, E])
        so_far = [sb(f"so_far_{i}", [P, E], BF16) for i in range(2)]
        place_of = sb("place_of", [P, GT, E])
        pad_rows = sb("pad_rows", [P, ROW])
        multiples = sb("multiples", [1, E, TILES + 1])
        tile_no = sb("tile_no", [1, LATER, E])
        tile_row = sb("tile_row", [1, LATER])
        ones_e = sb("ones_e", [1, E])
        expert = sb("expert", [1, LATER])
        weights_at = sb("weights_at", [1, TABLE], I32)
        tile_at = sb("tile_at", [1, TABLE], I32)
        first_counts = sb("first_counts", [1, E])
        first_full = sb("first_full", [1, E, FIRST_TILES])
        first_n = sb("first_n", [1, E])
        first_end = sb("first_end", [1, E + 1])
        first_passed = sb("first_passed", [1, FIRST_TILES, E])
        first_moved = sb("first_moved", [1, FIRST_TILES, E])
        first_tile = sb("first_tile", [1, FIRST_TILES])
        first_row = sb("first_row", [1, FIRST_TILES])
        end_capped = sb("end_capped", [1, E + 1])
        taken = sb("taken", [1, E + 1])
        taken_step = sb("taken_step", [1, E])
        region_step = sb("region_step", [1, E])
        later_row = sb("later_row", [1, LATER])
        counts = sb("counts", [1, E])
        pad_at = sb("pad_at", [1, E], I32)
        full = sb("full", [1, E, TILES])
        n_tiles = sb("n_tiles", [1, E])
        left = sb("left", [1, E])
        end_tile = sb("end_tile", [1, E])
        passed = sb("passed", [1, LATER, E])
        row_step = sb("row_step", [1, E])
        moved = sb("moved", [1, LATER, E])
        moved_rows = sb("moved_rows", [1, LATER])
        tok = [sb(f"tok_{i}", [P, ROW]) for i in range(RING + FIRST_TILES)]
        tokn = [sb(f"tokn_{i}", [P, D]) for i in range(2)]
        toknT = [sb(f"toknT_{i}", [P, P]) for i in range(2)]
        w1_now = [sb(f"w1_now_{i}", [P, F]) for i in range(2)]
        hT = [sb(f"hT_{i}", [P, F]) for i in range(2)]

        bank_xT = stack.enter_context(nc.psum_tensor("bank_xT", [P, 512], F32))
        bank_r = stack.enter_context(nc.psum_tensor("bank_r", [P, 512], F32))
        bank_q = stack.enter_context(nc.psum_tensor("bank_q", [P, 512], F32))
        bank_s = stack.enter_context(nc.psum_tensor("bank_s", [P, 512], F32))
        bank_p = stack.enter_context(nc.psum_tensor("bank_p", [P, 512], F32))
        bank_m = stack.enter_context(nc.psum_tensor("bank_m", [P, 512], F32))
        banks_o = stack.enter_context(nc.psum_tensor("banks_o", [P, 2, 512], F32))
        s_ps = bank_s[:, 0:GT * S].rearrange("p (t k) -> p t k", t=GT)
        lg_ps = bank_r[:, 0:GT * E].rearrange("p (t e) -> p t e", t=GT)
        pf_ps = bank_r[:, GT * E:2 * GT * E].rearrange("p (t e) -> p t e", t=GT)
        last_lg_ps = bank_s[:, 0:GT * E].rearrange("p (t e) -> p t e", t=GT)
        first_cnt_ps, cnt_ps = bank_q[:, 0:E], bank_s[:, 0:E]
        o_ps = banks_o[:, :, 0:2 * (D + 1)].rearrange("p b (t c) -> p b t c", c=D + 1)
        wT_ps, wkT_ps = bank_p[:, 0:D], bank_p[:, D:D + KA]
        wqk_ps, bqk_ps, wr_mean_ps = bank_m[:, 0:KA], bank_m[0:KA, KA:KA + 1], bank_r[:, 0:E]
        tT_ps = [bank_xT[:, 0:P], bank_m[:, 0:P]]
        h_ps = [bank_q, bank_p]
        y_ps = [banks_o[:, 0, 0:D], banks_o[:, 1, 0:D]]

        x_in = [sem(f"x_in{i}") for i in range(len(STATS1))]
        ctx_in_sem = [sem("ctx_in0"), sem("ctx_in1")]
        fold_w_in, gates_in, value_w_in, route_w_in, expert_w_in = (
            sem("fold_w_in"), sem("gates_in"), sem("value_w_in"), sem("route_w_in"), sem("expert_w_in"))
        zeroed, consts_ready, ids_ready, table_consts = (
            sem("zeroed"), sem("consts_ready"), sem("ids_ready"), sem("table_consts"))
        gates_ready, wv_ready = sem("gates_ready"), sem("wv_ready")
        wr_mean_done, wr_ready = sem("wr_mean_done"), sem("wr_ready")
        wT_ready, wT_copied, folded, folded_copied = (
            sem("wT_ready"), sem("wT_copied"), sem("folded"), sem("folded_copied"))
        def stages(*names):
            return [sem(n) for n in names]

        by_dve = shifted_ready, x2_ready, ln2_stats, logits_ready, onehot_ready, placed = stages(
            "shifted_ready", "x2_ready", "ln2_stats", "logits_ready", "onehot_ready", "placed")
        by_act = xn_ready, xnT_copied, ctxT_copied, qT_copied, probs_ready, probsT_copied, mixT_copied, x2T_copied, \
            exp_ready = stages("xn_ready", "xnT_copied", "ctxT_copied", "qT_copied", "probs_ready", "probsT_copied",
                               "mixT_copied", "x2T_copied", "exp_ready")
        by_pe = xnT_done, ctxT_done, qT_done, scores_done, probsT_done, mix_done, attn_done, x2T_done, \
            logits_done, prefix_done = stages("xnT_done", "ctxT_done", "qT_done", "scores_done", "probsT_done",
                                              "mix_done", "attn_done", "x2T_done", "logits_done", "prefix_done")
        by_pool = (rstd2_ready,) = stages("rstd2_ready")
        ln1_stats, norm1_ready = sem("ln1_stats"), sem("norm1_ready")
        first_scattered, scattered = sem("first_scattered"), sem("scattered")
        bn1, bn2, aggregated, max_done, sums_done, scaled_done, routing, recip_done, place_done = (
            sem("bn1"), sem("bn2"), sem("aggregated"), sem("max_done"), sem("sums_done"), sem("scaled_done"),
            sem("routing"), sem("recip_done"), sem("place_done"))
        ROUTING = 7
        eps1, pow1 = sem("eps1"), sem("pow1")
        wait_over, spare_written = sem("wait_over"), sem("spare_written")
        first_counts_done, first_table_ready = sem("first_counts_done"), sem("first_table_ready")
        counts_done, counts_copied, pad_at_ready, table_step, table_ready, pads_written = (
            sem("counts_done"), sem("counts_copied"), sem("pad_at_ready"), sem("table_step"),
            sem("table_ready"), sem("pads_written"))
        pads_ready = sem("pads_ready")
        tok_in = [sem(f"tok_in{i}") for i in range(RING + FIRST_TILES)]
        tok_out = [sem(f"tok_out{i}") for i in range(RING + FIRST_TILES)]
        ffn_dve = tokn_ready, toknT_copied, y_added = stages("tokn_ready", "toknT_copied", "y_added")
        ffn_pe = toknT_done, h_done, y_done = stages("toknT_done", "h_done", "y_done")
        gelu_done, w1_copied = sem("gelu_done"), sem("w1_copied")

        def steps(eng, body, tail):
            for k in range(LEAD):
                body(k, k // 2, k % 2)
            with eng.Fori(LEAD // 2, NG // 2) as i:
                for u in (0, 1):
                    body(i * 2 + u, i, u)
            body(NG, NG // 2, 0)
            tail()

        def x_of(g, t):
            return x_all[:, bass.ds(g * (GT * D) + t * D, D)]

        def live(k, lag):
            return not isinstance(k, int) or 0 <= k - lag < NG

        def tiles(eng, body, iteration=None):
            for j in range(FIRST_TILES):
                if iteration and j % RING == 0:
                    iteration(j // RING)
                body(j, j // RING, j % RING)
            with eng.Fori(FIRST_LOOPS, LOOPS) as i:
                if iteration:
                    iteration(i)
                for u in range(RING):
                    body(i * RING + u, i, u)
            if iteration:
                iteration(LOOPS)
            for j in range(LOOPS * RING, FFN_TILES):
                body(j, LOOPS, j % RING)

        def is_first(i):
            return isinstance(i, int) and i < FIRST_LOOPS

        def slot(i, u):
            return RING + i * RING + u if is_first(i) else u

        def uses(i):
            return 1 if is_first(i) else i - (FIRST_LOOPS - 1)

        def give_credit(eng, sems):
            for s in sems:
                eng.sem_inc(s, CREDIT)

        def wait_apart(eng, s, count):
            eng.wait_ge(s, count)
            eng.sem_inc(wait_over, 1)

        block = stack.enter_context(nc.Block())

        @block.sync
        def _(sp):
            def load_x(i):
                g0, g1 = STATS1[i]
                sp.dma_start(x_all[:, g0 * GT * D:g1 * GT * D].rearrange("p (t d) -> p t d", d=D),
                             x_tok[:, g0 * GT:g1 * GT, :]).then_inc(x_in[i], 16)

            def load_ctx(g, p):
                sp.dma_start(ctx_sb[p][:, :, 0:KD], ctx_tok[:, bass.ds(g * GT, GT), :]).then_inc(ctx_in_sem[p], 16)

            def load_expert(e):
                sp.dma_start(w1_sb[:, bass.ds(e * F, F)], W1.rearrange("e p f -> p e f")[:, bass.ds(e, 1), :]
                             .rearrange("p a f -> p (a f)")).then_inc(expert_w_in, 16)
                sp.dma_start(w2_sb[:, bass.ds(e * F, F)].rearrange("p (c d) -> p c d", d=D),
                             W2.rearrange("e (c p) d -> p (e c) d", p=P)[:, bass.ds(e * FC, FC), :]
                             ).then_inc(expert_w_in, 16)

            load_x(0)
            sp.dma_start(wq_sb[:], Wq).then_inc(fold_w_in, 16)
            sp.dma_start(wk_sb[0:KD, :], Wk).then_inc(fold_w_in, 16)
            sp.dma_start(wk_sb[KD:KA, :], bk.rearrange("(a d) -> a d", a=1)).then_inc(fold_w_in, 16)
            sp.dma_start(bq_col[:], bq.rearrange("(d a) -> d a", a=1)).then_inc(fold_w_in, 16)
            load_x(1)
            load_ctx(0, 0)
            sp.dma_start(gates[:, 0:1], g_xattn.partition_broadcast(P)).then_inc(gates_in, 16)
            sp.dma_start(gates[:, 1:2], g_ffn.partition_broadcast(P)).then_inc(gates_in, 16)
            sp.dma_start(wv_sb[0:KD, :], Wv).then_inc(value_w_in, 16)
            sp.dma_start(wv_sb[KD:KA, :], bv.rearrange("(a d) -> a d", a=1)).then_inc(value_w_in, 16)
            load_ctx(1, 1)
            sp.dma_start(wr_sb[:], Wr).then_inc(route_w_in, 16)
            sp.dma_start(br_sb[:], br.partition_broadcast(P)).then_inc(route_w_in, 16)
            load_x(2)
            load_x(3)
            load_expert(0)
            load_x(4)
            for e in range(1, E - NG + 2):
                load_expert(e)
            with sp.Fori(1, NG // 2) as i:
                for u in (0, 1):
                    g = i * 2 + u
                    sp.wait_ge(mix_done, nth(g - 2))
                    load_ctx(g, u)
                    load_expert(g + (E - NG))
            sp.wait_ge(pads_ready, 1)
            sp.dma_start(scratch[E * REGION:E * REGION + SPARE * P, :].rearrange("(t p) c -> p t c", p=P),
                         pad_rows[:].unsqueeze(1).broadcast_to([P, SPARE, ROW])).then_inc(spare_written, 16)

            at_regs = [sp.alloc_register(f"tile{m}") for m in range(RING)]

            def load_tiles(i, n, again):
                sp.reg_load(at_regs[0:n], tile_at[0:1, bass.ds(i * RING, n)])
                for u, r in enumerate(at_regs[0:n]):
                    at = sp.snap(r, min_val=0, max_val=E * REGION + (SPARE - 1) * P)
                    if again:
                        sp.wait_ge(tok_out[u], uses(i) * 16 - 16)
                    sp.dma_start(tok[slot(i, u)][:], scratch[bass.ds(at, P), :]).then_inc(tok_in[slot(i, u)], 16)

            sp.wait_ge(first_table_ready, 1)
            sp.wait_ge(first_scattered, 16 * GT * FIRST_GROUPS)
            for i in range(FIRST_LOOPS):
                load_tiles(i, RING, False)
            sp.wait_ge(pad_at_ready, 1)
            pad_regs = [sp.alloc_register(f"pad{e}") for e in range(E)]
            sp.reg_load(pad_regs, pad_at[0:1, :])
            for e, reg in enumerate(pad_regs):
                at = sp.snap(reg, min_val=e * REGION, max_val=e * REGION + N)
                sp.dma_start(scratch[bass.ds(at, P), :], pad_rows[:]).then_inc(pads_written, 16)
            sp.wait_ge(table_ready, 1)
            sp.wait_ge(scattered, 16 * GT * (NG - FIRST_GROUPS))
            sp.wait_ge(spare_written, 16)
            sp.wait_ge(pads_written, 16 * E)
            load_tiles(FIRST_LOOPS, RING, False)
            with sp.Fori(FIRST_LOOPS + 1, LOOPS) as i:
                load_tiles(i, RING, True)
            load_tiles(LOOPS, FFN_TILES - LOOPS * RING, True)
            for u in range(RING):
                sp.wait_ge(tok_out[u], 16 * (LOOPS - FIRST_LOOPS + (u < FFN_TILES - LOOPS * RING)))
            for j in range(FIRST_TILES):
                sp.wait_ge(tok_out[RING + j], 16)

        @block.gpsimd
        def _(pool):
            give_credit(pool, by_pool)
            nc.gpsimd.memset(ident[:], 0.0).then_inc(zeroed, 1)
            nc.gpsimd.memset(minus_half[:], -0.5)
            nc.gpsimd.memset(before[:], 0.0)
            nc.gpsimd.memset(averaging[:], 1.0 / D).then_inc(zeroed, 1)
            pool.wait_ge(zeroed, 1)
            nc.gpsimd.affine_select(out=ident[:], in_=ident[:], compare_op=ALU.not_equal, fill=1.0, base=0,
                                    pattern=[[-1, P]], channel_multiplier=1)
            nc.gpsimd.memset(ctx_sb[0][:, :, KD:KA], 1.0)
            nc.gpsimd.memset(ctx_sb[1][:, :, KD:KA], 1.0).then_inc(consts_ready, 1)

            def norm1(i):
                g0, g1 = STATS1[i]
                mean, var = (mv1[:, g0 * GT:g1 * GT, c:c + 1] for c in (0, 1))
                pool.wait_ge(ln1_stats, i + 1)
                nc.gpsimd.tensor_scalar(var, var, LN_EPS, None, ALU.add).then_inc(eps1, 1)
                nc.gpsimd.tensor_scalar(mean, mean, -1.0, None, ALU.mult)
                pool.wait_ge(eps1, i + 1)
                nc.gpsimd.tensor_tensor(var, var, minus_half[:, 0:(g1 - g0) * GT].unsqueeze(2), ALU.pow
                                        ).then_inc(pow1, 1)
                pool.wait_ge(pow1, i + 1)
                nc.gpsimd.tensor_tensor(mean, mean, var, ALU.mult).then_inc(norm1_ready, 1)

            nc.gpsimd.memset(probs[0][:], 0.0)
            nc.gpsimd.memset(probs[1][:], 0.0).then_inc(consts_ready, 1)
            pool.wait_ge(zeroed, 2)
            nc.gpsimd.affine_select(out=before[:], in_=before[:], compare_op=ALU.is_ge, fill=1.0, base=0,
                                    pattern=[[-1, P]], channel_multiplier=1)
            nc.gpsimd.memset(ones_b[:], 1.0)
            nc.gpsimd.memset(so_far[0][:], 0.0)
            nc.gpsimd.iota(region_part[:], [[0, GT], [REGION // P, E]], base=0, channel_multiplier=0,
                           allow_small_or_imprecise_dtypes=True)
            nc.gpsimd.iota(first_wins[:], [[0, GT], [-1, E]], base=E, channel_multiplier=0,
                           allow_small_or_imprecise_dtypes=True).then_inc(consts_ready, 1)
            norm1(0)
            norm1(1)
            nc.gpsimd.iota(rows[:, :, TOKEN:ROW].bitcast(I32), [[P, TILES]], base=0, channel_multiplier=1
                           ).then_inc(ids_ready, 1)
            nc.gpsimd.memset(pad_rows[:, 0:TOKEN], 0.0)
            nc.gpsimd.iota(pad_rows[:, TOKEN:ROW].bitcast(I32), [[0, 1]], base=N,
                           channel_multiplier=0).then_inc(pads_ready, 1)
            norm1(2)
            nc.gpsimd.iota(multiples[:], [[0, E], [P, TILES + 1]], base=0, channel_multiplier=0,
                           allow_small_or_imprecise_dtypes=True)
            norm1(3)
            nc.gpsimd.iota(tile_no[:], [[1, LATER], [0, E]], base=0, channel_multiplier=0,
                           allow_small_or_imprecise_dtypes=True)
            norm1(4)
            nc.gpsimd.iota(tile_row[:], [[P, LATER]], base=0, channel_multiplier=0,
                           allow_small_or_imprecise_dtypes=True)
            nc.gpsimd.iota(region_of[:], [[REGION, E]], base=0, channel_multiplier=0,
                           allow_small_or_imprecise_dtypes=True)
            nc.gpsimd.memset(first_end[:, 0:1], 0.0)
            nc.gpsimd.memset(taken[:, E:E + 1], 0.0)
            nc.gpsimd.memset(ones_e[:], 1.0).then_inc(table_consts, 1)

            def norm2(g):
                mean, var = mv2[g % 2][:, :, 0:1], mv2[g % 2][:, :, 1:2]
                rstd = rows[:, g * GT:(g + 1) * GT, RSTD:SCALE]
                pool.wait_ge(aggregated, g + 1)
                nc.gpsimd.tensor_copy(rows[:, g * GT:(g + 1) * GT, MEAN:RSTD], mean)
                pool.wait_ge(ln2_stats, nth(g))
                nc.gpsimd.tensor_tensor(rstd, var, minus_half[:, 0:GT].unsqueeze(2), ALU.pow).then_inc(rstd2_ready, 1)

            def scatter_rows(g, tiles):
                pool.wait_ge(placed, nth(g))
                for t in tiles:
                    nc.gpsimd.indirect_dma_start(
                        out=scratch, out_offset=bass.IndirectOffsetOnAxis(ap=row_at[:, g * GT + t:g * GT + t + 1], axis=0),
                        in_=rows[:, g * GT + t, :], in_offset=None
                        ).then_inc(first_scattered if g < FIRST_GROUPS else scattered, 16)

            pool.wait_ge(ids_ready, 1)
            norm2(0)
            for g in range(1, NG - 1):
                norm2(g)
                if g == NG - 2:
                    norm2(g + 1)
                pool.wait_ge(rstd2_ready, nth(g - 1))
                scatter_rows(g - 1, range(GT))
            pool.wait_ge(rstd2_ready, nth(NG - 1))
            scatter_rows(NG - 2, range(GT))
            scatter_rows(NG - 1, range(GT))

            def scatter_tile(j, i, u):
                wait_apart(pool, y_added, nth(j))
                v = slot(i, u)
                nc.gpsimd.indirect_dma_start(
                    out=out_tok, out_offset=bass.IndirectOffsetOnAxis(ap=tok[v][:, TOKEN:ROW].bitcast(I32), axis=0),
                    in_=tok[v][:, 0:D], in_offset=None, bounds_check=N - 1, oob_is_err=False).then_inc(tok_out[v], 16)

            tiles(pool, scatter_tile)

        @block.scalar
        def _(act):
            give_credit(act, by_act)
            act.sem_inc(gelu_done, CREDIT)
            act.wait_ge(gates_in, 32)
            nc.scalar.activation(tanh_gates[:], gates[:], ACT.Tanh).then_inc(gates_ready, 1)

            w_regs = [act.alloc_register(f"wa{m}") for m in range(TW)]
            w_at = []

            def experts_of(i, n=TW):
                act.reg_load(w_regs[0:n], weights_at[0:1, bass.ds(i * RING, n)])
                w_at[:] = [act.snap(r, min_val=0, max_val=(E - 1) * F) for r in w_regs[0:n]]

            def copy_w1(u):
                nc.scalar.copy(w1_now[u % 2][:], w1_sb[:, bass.ds(w_at[u], F)]).then_inc(w1_copied, 1)

            def evacuate(dst, src, filled, freed, copied, g):
                act.wait_ge(filled, nth(g))
                act.wait_ge(freed, nth(g - 2))
                nc.scalar.copy(dst, src).then_inc(copied, 1)

            def normalise1(g, p):
                last_range = max(i for i, (g0, g1) in enumerate(STATS1) if not isinstance(g, int) or g0 <= g)
                act.wait_ge(norm1_ready, last_range + 1)
                act.wait_ge(xnT_done, nth(g - 2))
                mv_flat = mv1[:].rearrange("p t c -> p (t c)")
                for t in range(GT):
                    def stat(c):
                        return mv_flat[:, bass.ds(g * (GT * 2) + (t * 2 + c), 1)]

                    last = nc.scalar.activation(xn[p][:, t, :], x_of(g, t), ACT.Identity, bias=stat(0), scale=stat(1))
                last.then_inc(xn_ready, 1)

            def copy_qT(g, p):
                act.wait_ge(qT_done, nth(g))
                act.wait_ge(scores_done, nth(g - 2))
                nc.scalar.activation(qT[p][:], bank_q[0:KA, :], ACT.Identity, bias=bqk_sb[:, 0:1]
                                     ).then_inc(qT_copied, 1)

            def copy_probsT(g, p):
                evacuate(probsT[p][:], bank_p[:], probsT_done, mix_done, probsT_copied, g)

            def copy_mixT(g, p):
                evacuate(mixT[p][:], bank_m[0:KA, :], mix_done, attn_done, mixT_copied, g)

            def copy_x2T(g, p):
                evacuate(x2T[p][:], bank_p[:], x2T_done, logits_done, x2T_copied, g)

            def exp_scores(g, p):
                act.wait_ge(shifted_ready, nth(g))
                act.wait_ge(probsT_done, nth(g - 2))
                nc.scalar.activation(probs[p][0:S, :, 0:S], shifted[p][0:S], ACT.Exp)
                nc.scalar.activation(probs[p][S:P, :, S:P], shifted[p][S:P], ACT.Exp).then_inc(probs_ready, 1)

            def exp_logits(g, exp_neg):
                act.wait_ge(logits_ready, nth(g))
                nc.scalar.activation(exp_neg[:], logits[:], ACT.Exp, scale=-1.0).then_inc(exp_ready, 1)

            def body(k, i, u):
                v = 1 - u
                if live(k, 1):
                    evacuate(xnT[v][:], bank_xT[:], xnT_done, qT_done, xnT_copied, k - 1)
                if live(k, 2):
                    copy_probsT(k - 2, u)
                if live(k, 1):
                    copy_qT(k - 1, v)
                    evacuate(ctxT[v][:], bank_xT[0:KA, :], ctxT_done, scores_done, ctxT_copied, k - 1)
                if live(k, 3):
                    copy_x2T(k - 3, v)
                if live(k, 2):
                    copy_mixT(k - 2, u)
                if live(k, 0):
                    normalise1(k, u)
                if live(k, 1):
                    exp_scores(k - 1, v)
                if live(k, 3):
                    act.wait_ge(onehot_ready, nth(k - 4))
                    exp_logits(k - 3, exp_neg)

            def tail():
                copy_probsT(NG - 1, 1)
                copy_mixT(NG - 1, 1)
                copy_x2T(NG - 2, 0)
                copy_x2T(NG - 1, 1)
                act.wait_ge(onehot_ready, nth(NG - 3))
                exp_logits(NG - 2, exp_neg)
                act.wait_ge(expert_w_in, 16 * 2 * E)
                act.wait_ge(first_table_ready, 1)
                experts_of(0)
                copy_w1(0)
                copy_w1(1)
                exp_logits(NG - 1, exp_neg_last)
                nc.scalar.activation(gelu_table[:], tanh_gates[:], ACT.Gelu)

            act.wait_ge(consts_ready, 2)
            act.wait_ge(folded_copied, 2)
            steps(act, body, tail)

            def gelu(j, i, u):
                act.wait_ge(h_done, nth(j))
                act.wait_ge(y_done, nth(j - 2))
                nc.scalar.activation(hT[u % 2][:], h_ps[u % 2][:], ACT.Gelu).then_inc(gelu_done, 1)
                if isinstance(j, int) and j == FIRST_TILES - 3:
                    act.wait_ge(table_ready, 1)
                    experts_of(FIRST_LOOPS - 1)
                if not isinstance(j, int) or j + 2 < FFN_TILES:
                    copy_w1(u + 2)

            def look_up_experts(i):
                if not isinstance(i, int) or i > 0:
                    experts_of(i, RING if isinstance(i, int) and i == FIRST_LOOPS - 1 else TW)

            tiles(act, gelu, iteration=look_up_experts)

        @block.vector
        def _(dve):
            give_credit(dve, by_dve)
            give_credit(dve, ffn_dve)

            def fold_weights():
                dve.wait_ge(wT_ready, 1)
                nc.vector.tensor_copy(wqT_sb[:], wT_ps)
                nc.vector.tensor_copy(wkT_sb[:], wkT_ps).then_inc(wT_copied, 1)
                dve.wait_ge(folded, 1)
                nc.vector.tensor_copy(wqk_sb[:], wqk_ps).then_inc(folded_copied, 1)
                nc.vector.tensor_copy(bqk_sb[:], bqk_ps).then_inc(folded_copied, 1)

            def scale_weights():
                dve.wait_ge(value_w_in, 32)
                dve.wait_ge(gates_ready, 1)
                nc.vector.tensor_scalar(wvg_sb[:, 0:D], wv_sb[:], tanh_gates[0:KA, 0:1], None, ALU.mult)
                nc.vector.memset(wvg_sb[0:KD, D:D + 1], 0.0)
                nc.vector.memset(wvg_sb[KD:KA, D:D + 1], 1.0).then_inc(wv_ready, 1)
                dve.wait_ge(route_w_in, 32)
                dve.wait_ge(wr_mean_done, 1)
                nc.vector.tensor_tensor(wr_centred[:], wr_sb[:], wr_mean_ps, ALU.subtract).then_inc(wr_ready, 1)

            def layer_stats1(i):
                g0, g1 = STATS1[i]
                dve.wait_ge(x_in[i], 16)
                for t in range(g0 * GT, g1 * GT):
                    last = nc.vector.bn_stats(stats1[:, t, :], x_of(0, t))
                last.then_inc(bn1, 1)
                dve.wait_ge(bn1, i + 1)
                for t in range(g0 * GT, g1 * GT):
                    last = nc.vector.bn_aggr(mv1[:, t, :], stats1[:, t, :])
                last.then_inc(ln1_stats, 1)

            def softmax_shift(g, p):
                dve.wait_ge(scores_done, nth(g))
                nc.vector.tensor_reduce(rowmax[:], s_ps, AX.X, ALU.max).then_inc(max_done, 1)
                dve.wait_ge(max_done, g + 1)
                dve.wait_ge(probs_ready, nth(g - 2))
                nc.vector.tensor_tensor(shifted[p][:], s_ps, rowmax[:].unsqueeze(2).broadcast_to([P, GT, S]),
                                        ALU.subtract).then_inc(shifted_ready, 1)

            def layer_stats2(g, p):
                dve.wait_ge(x2_ready, nth(g))
                for t in range(GT):
                    last = nc.vector.bn_stats(stats2[:, t, :], x2[p][:, t, :])
                last.then_inc(bn2, 1)

            def aggregate_stats2(g, p):
                wait_apart(dve, bn2, g + 1)
                wait_apart(dve, rstd2_ready, nth(g - 2))
                for t in range(GT):
                    last = nc.vector.bn_aggr(mv2[p][:, t, :], stats2[:, t, :])
                last.then_inc(aggregated, 1)
                dve.wait_ge(aggregated, g + 1)
                nc.vector.tensor_scalar(mv2[p][:, :, 1:2], mv2[p][:, :, 1:2], LN_EPS, None, ALU.add
                                        ).then_inc(ln2_stats, 1)
                nc.vector.tensor_copy(rows[:, bass.ds(g * GT, GT), 0:D], x2[p][:])

            def column(g, c):
                return rows[:, bass.ds(g * GT, GT), c:c + 1]

            def route_logits(g, lg_ps=lg_ps):
                wide = [P, GT, E]
                dve.wait_ge(logits_done, nth(g))
                dve.wait_ge(rstd2_ready, nth(g))
                nc.vector.tensor_tensor(scaled[:], lg_ps, column(g, RSTD).broadcast_to(wide), ALU.mult
                                        ).then_inc(scaled_done, 1)
                dve.wait_ge(scaled_done, g + 1)
                dve.wait_ge(exp_ready, nth(g - 1))
                nc.vector.tensor_tensor(logits[:], scaled[:], br_sb[:].unsqueeze(1).broadcast_to(wide), ALU.add
                                        ).then_inc(logits_ready, 1)

            def residual_and_choose(k, u, adds, chooses, copies=(), exp_neg=exp_neg):
                r, g, p = k - 2, k - 3, 1 - u
                wide = [P, GT, E]

                def residual(t):
                    if adds:
                        last = nc.vector.scalar_tensor_tensor(
                            out=x2[u][:, t, :], in0=o_ps[:, t // 2, t % 2, 0:D],
                            scalar=inv_sum[:, t // 2, t % 2, :], in1=x_of(r, t), op0=ALU.mult, op1=ALU.add)
                        if t == GT - 1:
                            last.then_inc(x2_ready, 1)
                    elif t >= GT - len(copies):
                        j = copies[t - GT]
                        copy_transposed(j, j % 2)

                if chooses:
                    dve.wait_ge(exp_ready, nth(g))
                    nc.vector.tensor_scalar(one_plus[:], exp_neg[:], 1.0, None, ALU.add).then_inc(routing, 1)
                    dve.wait_ge(routing, g * ROUTING + 1)
                    nc.vector.tensor_reduce(least[:], one_plus[:], AX.X, ALU.min).then_inc(routing, 1)
                if adds:
                    dve.wait_ge(attn_done, nth(r))
                    dve.wait_ge(x2T_done, nth(r - 2))
                    nc.vector.reciprocal(inv_sum[:], o_ps[:, :, :, D:D + 1]).then_inc(sums_done, 1)
                if chooses:
                    dve.wait_ge(routing, g * ROUTING + 2)
                    nc.vector.tensor_tensor(is_max[:], one_plus[:], least[:].broadcast_to(wide), ALU.is_equal
                                            ).then_inc(routing, 1)
                if adds:
                    dve.wait_ge(sums_done, r + 1)
                residual(0)
                if chooses:
                    dve.wait_ge(routing, g * ROUTING + 3)
                    nc.vector.tensor_tensor(rank_max[:], is_max[:], first_wins[:], ALU.mult).then_inc(routing, 1)
                residual(1)
                if chooses:
                    dve.wait_ge(routing, g * ROUTING + 4)
                    nc.vector.tensor_reduce(best[:], rank_max[:], AX.X, ALU.max).then_inc(routing, 1)
                residual(2)
                if chooses:
                    dve.wait_ge(routing, g * ROUTING + 5)
                    dve.wait_ge(prefix_done, nth(g - 1))
                    nc.vector.tensor_tensor(onehot[p][:], rank_max[:], best[:].broadcast_to(wide), ALU.is_equal
                                            ).then_inc(routing, 1)
                residual(3)
                if chooses:
                    dve.wait_ge(routing, g * ROUTING + 6)
                    nc.vector.tensor_reduce(group_sum[:], onehot[p][:].rearrange("p t e -> p e t"), AX.X, ALU.add
                                            ).then_inc(routing, 1)
                    nc.vector.reciprocal(route_max[:], least[:]).then_inc(recip_done, 1)
                    dve.wait_ge(routing, g * ROUTING + 7)
                    nc.vector.tensor_tensor(so_far[1 - p][:], so_far[p][:], group_sum[:], ALU.add
                                            ).then_inc(onehot_ready, 1)
                    dve.wait_ge(recip_done, g + 1)
                    nc.vector.tensor_scalar(column(g, SCALE), route_max[:], tanh_gates[:, 1:2], None, ALU.mult)

            def place_rows(g, p):
                dve.wait_ge(prefix_done, nth(g))
                nc.vector.tensor_tensor(place_of[:], pf_ps, onehot[p][:], ALU.mult).then_inc(place_done, 1)
                dve.wait_ge(place_done, g + 1)
                with nc.allow_low_precision(reason="whole numbers below 2**24 are exact"):
                    nc.vector.tensor_reduce(row_at[:, bass.ds(g * GT, GT)], place_of[:], AX.X, ALU.add
                                            ).then_inc(placed, 1)

            def body(k, i, u):
                v = 1 - u
                if live(k, 3):
                    layer_stats2(k - 3, v)
                if live(k, 4):
                    place_rows(k - 4, u)
                if live(k, 3):
                    aggregate_stats2(k - 3, v)
                if live(k, 1):
                    softmax_shift(k - 1, v)
                if isinstance(k, int) and 1 <= k < len(STATS1) - 2:
                    layer_stats1(k + 2)
                if live(k, 3):
                    route_logits(k - 3)
                residual_and_choose(k, u, live(k, 2), live(k, 3))

            def tail():
                layer_stats2(NG - 2, 0)
                place_rows(NG - 3, 1)
                aggregate_stats2(NG - 2, 0)
                residual_and_choose(NG + 1, 1, True, False)
                find_first_tiles()
                place_first_tiles()
                route_logits(NG - 2)
                layer_stats2(NG - 1, 1)
                aggregate_stats2(NG - 1, 1)
                normalise_tile(0, 0, 0)
                normalise_tile(1, 0, 1)
                copy_transposed(0, 0)
                copy_transposed(1, 1)
                normalise_tile(2, 0, 2)
                route_logits(NG - 1, last_lg_ps)
                residual_and_choose(NG + 1, 1, False, True, copies=(2,))
                normalise_tile(3, 0, 3)
                place_rows(NG - 2, 0)
                residual_and_choose(NG + 2, 0, False, True, exp_neg=exp_neg_last)
                copy_transposed(3, 1)
                normalise_tile(4, 0, 4)
                count_taken_tiles()
                dve.wait_ge(counts_done, 1)
                nc.vector.tensor_copy(counts[:], cnt_ps[0:1, :]).then_inc(counts_copied, 1)
                dve.wait_ge(counts_copied, 1)
                nc.vector.tensor_tensor(pad_at[:], counts[:], region_of[:], ALU.add).then_inc(pad_at_ready, 1)
                place_rows(NG - 1, 1)

            table = [0]

            def link(ins):
                table[0] += 1
                ins.then_inc(table_step, 1)
                dve.wait_ge(table_step, table[0])

            def find_first_tiles():
                deep = [1, FIRST_TILES, E]
                dve.wait_ge(table_consts, 1)
                dve.wait_ge(first_counts_done, 1)
                link(nc.vector.tensor_copy(first_counts[:], first_cnt_ps[0:1, :]))
                link(nc.vector.tensor_tensor(first_full[:], first_counts[:].unsqueeze(2).broadcast_to([1, E, FIRST_TILES]),
                                             multiples[:, :, 1:FIRST_TILES + 1], ALU.is_ge))
                link(nc.vector.tensor_reduce(first_n[:], first_full[:], AX.X, ALU.add))
                link(nc.vector.tensor_tensor_scan(first_end[:, 1:E + 1], ones_e[:], first_n[:], 0.0,
                                                  ALU.mult, ALU.add))
                link(nc.vector.tensor_tensor(first_passed[:], first_end[:, 1:E + 1].unsqueeze(1).broadcast_to(deep),
                                             tile_no[:, 0:FIRST_TILES, :], ALU.is_le))

            def place_first_tiles():
                deep = [1, FIRST_TILES, E]
                nc.vector.tensor_tensor(first_moved[:], first_passed[:], first_n[:].unsqueeze(1).broadcast_to(deep),
                                        ALU.mult)
                link(nc.vector.tensor_reduce(expert[:, 0:FIRST_TILES], first_passed[:], AX.X, ALU.add))
                nc.vector.tensor_reduce(first_tile[:], first_moved[:], AX.X, ALU.add)
                nc.vector.tensor_scalar(weights_at[:, 0:FIRST_TILES], expert[:, 0:FIRST_TILES], float(F), None, ALU.mult)
                link(nc.vector.scalar_tensor_tensor(out=first_row[:], in0=expert[:, 0:FIRST_TILES], scalar=float(REGION),
                                                    in1=tile_row[:, 0:FIRST_TILES], op0=ALU.mult, op1=ALU.add))
                nc.vector.scalar_tensor_tensor(out=tile_at[:, 0:FIRST_TILES], in0=first_tile[:], scalar=float(-P),
                                               in1=first_row[:], op0=ALU.mult, op1=ALU.add
                                               ).then_inc(first_table_ready, 1)

            def count_taken_tiles():
                link(nc.vector.tensor_scalar(end_capped[:], first_end[:], float(FIRST_TILES), None, ALU.min))
                link(nc.vector.tensor_tensor(taken[:, 0:E], end_capped[:, 1:E + 1], end_capped[:, 0:E],
                                             ALU.subtract))
                nc.vector.scalar_tensor_tensor(out=later_row[:], in0=taken[:, 0:1].broadcast_to([1, LATER]),
                                               scalar=float(P), in1=tile_row[:], op0=ALU.mult, op1=ALU.add)
                link(nc.vector.tensor_tensor(taken_step[:], taken[:, 1:E + 1], taken[:, 0:E], ALU.subtract))
                link(nc.vector.tensor_scalar(region_step[:], taken_step[:], float(P), float(REGION),
                                             ALU.mult, ALU.add))

            def find_later_tiles():
                link(nc.vector.tensor_tensor(full[:], counts[:].unsqueeze(2).broadcast_to([1, E, TILES]),
                                             multiples[:, :, 0:TILES], ALU.is_gt))
                link(nc.vector.tensor_reduce(n_tiles[:], full[:], AX.X, ALU.add))

            def sum_tiles():
                link(nc.vector.tensor_tensor(left[:], n_tiles[:], taken[:, 0:E], ALU.subtract))
                nc.vector.scalar_tensor_tensor(out=row_step[:], in0=left[:], scalar=float(-P), in1=region_step[:],
                                               op0=ALU.mult, op1=ALU.add)
                link(nc.vector.tensor_tensor_scan(end_tile[:], ones_e[:], left[:], 0.0, ALU.mult, ALU.add))

            def pass_experts():
                deep = [1, LATER, E]
                link(nc.vector.tensor_tensor(passed[:], end_tile[:].unsqueeze(1).broadcast_to(deep), tile_no[:],
                                             ALU.is_le))
                link(nc.vector.tensor_tensor(moved[:], passed[:], row_step[:].unsqueeze(1).broadcast_to(deep),
                                             ALU.mult))

            def place_later_tiles():
                nc.vector.tensor_reduce(moved_rows[:], moved[:], AX.X, ALU.add)
                link(nc.vector.tensor_reduce(expert[:], passed[:], AX.X, ALU.add))
                nc.vector.tensor_tensor(tile_at[:, FIRST_TILES:TABLE], moved_rows[:], later_row[:], ALU.add)
                nc.vector.tensor_scalar(weights_at[:, FIRST_TILES:TABLE], expert[:], float(E - 1), float(F), ALU.min,
                                        ALU.mult).then_inc(table_ready, 1)

            LATER_TABLE = (find_later_tiles, sum_tiles, pass_experts, place_later_tiles)

            def normalise_tile(j, i, u):
                v = slot(i, u)
                dve.wait_ge(tok_in[v], uses(i) * 16)
                dve.wait_ge(toknT_done, nth(j - 2))
                nc.vector.tensor_scalar(tokn[u % 2][:], tok[v][:, 0:D], tok[v][:, MEAN:RSTD], tok[v][:, RSTD:SCALE],
                                        ALU.subtract, ALU.mult).then_inc(tokn_ready, 1)

            def copy_transposed(j, u):
                dve.wait_ge(toknT_done, nth(j))
                dve.wait_ge(h_done, nth(j - 2))
                nc.vector.tensor_copy(toknT[u % 2][:], tT_ps[u % 2]).then_inc(toknT_copied, 1)

            def residual2(j, i, u):
                tile = tok[slot(i, u)]
                dve.wait_ge(y_done, nth(j))
                nc.vector.scalar_tensor_tensor(out=tile[:, 0:D], in0=y_ps[u % 2], scalar=tile[:, SCALE:TOKEN],
                                               in1=tile[:, 0:D], op0=ALU.mult, op1=ALU.add).then_inc(y_added, 1)

            def tile(j, i, u):
                if not isinstance(j, int) or 2 <= j and j + 2 < FFN_TILES:
                    copy_transposed(j + 2, u + 2)
                    if not isinstance(j, int) or j + 3 < FFN_TILES:
                        normalise_tile(j + 3, i + (u + 3) // RING, (u + 3) % RING)
                if isinstance(j, int) and 2 <= j < 2 + len(LATER_TABLE):
                    LATER_TABLE[j - 2]()
                residual2(j, i, u)

            layer_stats1(0)
            fold_weights()
            layer_stats1(1)
            scale_weights()
            layer_stats1(2)
            dve.wait_ge(consts_ready, 3)
            steps(dve, body, tail)

            tiles(dve, tile)

        @block.tensor
        def _(pe):
            give_credit(pe, by_pe)
            give_credit(pe, ffn_pe)
            def keep_busy(n):
                for _ in range(n):
                    nc.tensor.matmul(bank_s[:], ident[:], probs[0][:], start=True, stop=True)

            pe.wait_ge(consts_ready, 1)
            pe.wait_ge(consts_ready, 2)
            keep_busy(2)
            pe.wait_ge(fold_w_in, 16 * 4)
            nc.tensor.transpose(wT_ps, wq_sb[:], ident[:])
            nc.tensor.transpose(wkT_ps, wk_sb[:], ident[0:KA, 0:KA]).then_inc(wT_ready, 1)
            pe.wait_ge(wT_copied, 1)
            nc.tensor.matmul(wqk_ps, wqT_sb[:], wkT_sb[:], start=True, stop=True)
            nc.tensor.matmul(bqk_ps, wkT_sb[:], bq_col[:], start=True, stop=True).then_inc(folded, 1)

            keep_busy(1)
            pe.wait_ge(route_w_in, 32)
            pe.wait_ge(zeroed, 2)
            nc.tensor.matmul(wr_mean_ps, averaging[:], wr_sb[:], start=True, stop=True).then_inc(wr_mean_done, 1)

            def transposes(dst, src, done):
                for t in range(GT):
                    last = nc.tensor.transpose(dst[:, t * P:(t + 1) * P], src[t], ident[:])
                last.then_inc(done, 1)

            def scores(g, p):
                pe.wait_ge(qT_copied, nth(g))
                pe.wait_ge(ctxT_copied, nth(g))
                pe.wait_ge(shifted_ready, nth(g - 1))
                for t in range(GT):
                    for b in range(2):
                        cols = slice(t * P + b * S, t * P + b * S + S)
                        last = nc.tensor.matmul(s_ps[b * S:b * S + S, t, :], qT[p][:, cols], ctxT[p][:, cols],
                                                start=True, stop=True)
                last.then_inc(scores_done, 1)

            def prefix(g, p):
                pe.wait_ge(onehot_ready, nth(g))
                pe.wait_ge(placed, nth(g - 1))
                pe.wait_ge(consts_ready, 3)
                nc.tensor.matmul(pf_ps, before[:], onehot[p][:], start=True, stop=False)
                for t in range(GT - 1):
                    nc.tensor.matmul(pf_ps[:, t + 1:GT, :], ones_b[:],
                                     onehot[p][:, t:t + 1, :].broadcast_to([P, GT - 1 - t, E]),
                                     start=False, stop=False)
                nc.tensor.matmul(pf_ps, ones_b[:], region_part[:], start=False, stop=False)
                nc.tensor.matmul(pf_ps, ones_b[:], so_far[p][:].unsqueeze(1).broadcast_to([P, GT, E]),
                                 start=False, stop=True).then_inc(prefix_done, 1)

            def transpose_probs(g, p):
                pe.wait_ge(probs_ready, nth(g))
                pe.wait_ge(x2T_copied, nth(g - 2))
                transposes(bank_p, [probs[p][:, t, :] for t in range(GT)], probsT_done)

            def transpose_x2(g, p):
                pe.wait_ge(x2_ready, nth(g))
                pe.wait_ge(probsT_copied, nth(g + 1, NG - 1))
                pe.wait_ge(x2T_copied, nth(g - 1))
                transposes(bank_p, [x2[p][:, t, :] for t in range(GT)], x2T_done)

            def mix(g, p):
                pe.wait_ge(probsT_copied, nth(g))
                pe.wait_ge(mixT_copied, nth(g - 1))
                for t in range(GT):
                    last = nc.tensor.matmul(bank_m[0:KA, t * P:(t + 1) * P], ctx_sb[p][:, t, :],
                                            probsT[p][:, t * P:(t + 1) * P], start=True, stop=True)
                last.then_inc(mix_done, 1)

            def attend(g, p):
                pe.wait_ge(mixT_copied, nth(g))
                pe.wait_ge(x2_ready, nth(g - 1))
                for t in range(GT):
                    last = nc.tensor.matmul(o_ps[:, t // 2, t % 2, :], mixT[p][:, t * P:(t + 1) * P], wvg_sb[:],
                                            start=True, stop=True)
                last.then_inc(attn_done, 1)

            def route(g, p, lg_ps):
                pe.wait_ge(x2T_copied, nth(g))
                for t in range(GT):
                    last = nc.tensor.matmul(lg_ps[:, t, :], x2T[p][:, t * P:(t + 1) * P], wr_centred[:],
                                            start=(t == 0), stop=(t == GT - 1))
                last.then_inc(logits_done, 1)

            def body(k, i, u):
                v = 1 - u
                if live(k, 1):
                    pe.wait_ge(xn_ready, nth(k - 1))
                    pe.wait_ge(ctxT_copied, nth(k - 2))
                    transposes(bank_xT, [xn[v][:, t, :] for t in range(GT)], xnT_done)
                if live(k, 2):
                    transpose_probs(k - 2, u)
                if live(k, 1):
                    pe.wait_ge(xnT_copied, nth(k - 1))
                    pe.wait_ge(qT_copied, nth(k - 2))
                    nc.tensor.matmul(bank_q[0:KA, :], wqk_sb[:], xnT[v][:], start=True, stop=True).then_inc(qT_done, 1)
                    pe.wait_ge(ctx_in_sem[v], (i + u) * 16)
                    transposes(bank_xT[0:KA, :], [ctx_sb[v][:, t, :] for t in range(GT)], ctxT_done)
                if live(k, 4):
                    prefix(k - 4, u)
                if live(k, 3):
                    transpose_x2(k - 3, v)
                if live(k, 2):
                    mix(k - 2, u)
                if live(k, 1):
                    scores(k - 1, v)
                if isinstance(k, int) and k == 3:
                    pe.wait_ge(wr_ready, 1)
                if live(k, 3):
                    pe.wait_ge(placed, nth(k - 4))
                    route(k - 3, v, lg_ps)
                if isinstance(k, int) and k == 2:
                    pe.wait_ge(wv_ready, 1)
                if live(k, 2):
                    attend(k - 2, u)

            def transpose_tile(j, u):
                pe.wait_ge(tokn_ready, nth(j))
                pe.wait_ge(toknT_copied, nth(j - 2))
                nc.tensor.transpose(tT_ps[u % 2], tokn[u % 2][:], ident[:]).then_inc(toknT_done, 1)

            def up(j, u):
                pe.wait_ge(toknT_copied, nth(j))
                pe.wait_ge(w1_copied, j + 1)
                pe.wait_ge(gelu_done, nth(j - 2))
                for c in range(FC):
                    last = nc.tensor.matmul(h_ps[u % 2][:, c * P:(c + 1) * P], w1_now[u % 2][:, c * P:(c + 1) * P],
                                            toknT[u % 2][:], start=True, stop=True)
                last.then_inc(h_done, 1)

            def tail():
                pe.wait_ge(onehot_ready, nth(FIRST_GROUPS - 1))
                pe.wait_ge(qT_copied, nth(NG - 1))
                nc.tensor.matmul(first_cnt_ps, ones_b[:], so_far[FIRST_GROUPS % 2][:], start=True, stop=True
                                 ).then_inc(first_counts_done, 1)
                transpose_probs(NG - 1, 1)
                mix(NG - 1, 1)
                prefix(NG - 3, 1)
                transpose_x2(NG - 2, 0)
                attend(NG - 1, 1)
                pe.wait_ge(placed, nth(NG - 3))
                route(NG - 2, 0, lg_ps)
                transpose_x2(NG - 1, 1)
                pe.wait_ge(shifted_ready, nth(NG - 1))
                route(NG - 1, 1, last_lg_ps)
                transpose_tile(0, 0)
                transpose_tile(1, 1)
                up(0, 0)
                transpose_tile(2, 0)
                up(1, 1)
                prefix(NG - 2, 0)

            def end_routing():
                pe.wait_ge(onehot_ready, nth(NG - 1))
                pe.wait_ge(logits_ready, nth(NG - 1))
                nc.tensor.matmul(cnt_ps, ones_b[:], so_far[NG % 2][:], start=True, stop=True).then_inc(counts_done, 1)
                prefix(NG - 1, 1)

            steps(pe, body, tail)

            w_regs = [pe.alloc_register(f"w{m}") for m in range(RING)]
            w_at = []

            def experts_of(i):
                pe.reg_load(w_regs, weights_at[0:1, bass.ds(i * RING, RING)])
                w_at[:] = [pe.snap(r, min_val=0, max_val=(E - 1) * F) for r in w_regs]

            def down(j, u, at):
                pe.wait_ge(gelu_done, nth(j))
                pe.wait_ge(y_added, nth(j - 2))
                for c in range(FC):
                    last = nc.tensor.matmul(y_ps[u % 2], hT[u % 2][:, c * P:(c + 1) * P],
                                            w2_sb[:, bass.ds(at + c * D, D)], start=(c == 0), stop=(c == FC - 1))
                last.then_inc(y_done, 1)

            pe.wait_ge(expert_w_in, 16 * 2 * E)
            pe.wait_ge(first_table_ready, 1)

            def tile(j, i, u):
                if not isinstance(j, int) or 1 <= j and j + 2 < FFN_TILES:
                    transpose_tile(j + 2, u)
                if not isinstance(j, int) or 1 <= j and j + 1 < FFN_TILES:
                    up(j + 1, u + 1)
                if isinstance(j, int) and j == 1:
                    end_routing()
                down(j, u, w_at[u])
                if isinstance(j, int) and j == FIRST_TILES - 1:
                    pe.wait_ge(table_ready, 1)

            tiles(pe, tile, iteration=experts_of)


_INS = ["x", "ctx_512", "g_xattn", "g_ffn", "L0_xattn_Wq", "L0_xattn_bq", "L0_xattn_Wk", "L0_xattn_bk",
        "L0_xattn_Wv", "L0_xattn_bv", "L0_ffn_Wr", "L0_ffn_br", "L0_ffn_W1", "L0_ffn_W2"]


def kernel(**inputs):
    import numpy as _np
    import concourse.bacc as _bacc
    from concourse import mybir as _mybir
    from concourse.bass_utils import run_bass_kernel_spmd as _run

    nc = _bacc.Bacc("TRN2", target_bir_lowering=False, num_devices=1)
    arrays, args = {}, []
    for name in _INS:
        a = _np.ascontiguousarray(inputs[name])
        arrays[f"in_{name}_dram"] = a
        args.append(nc.dram_tensor(f"in_{name}_dram", a.shape, _mybir.dt.from_np(a.dtype), kind="ExternalInput").ap())
    shape = _np.shape(inputs["x"])
    args.append(nc.dram_tensor("out_0_dram", shape, _mybir.dt.float32, kind="ExternalOutput").ap())
    attention_moe(nc, *args)
    r = _run(nc, [arrays], core_ids=[0])
    return r.results[0]["out_0_dram"]
```
